# Optimizing a Trainium2 kernel written in Bass

```python
import numpy as np
import jax
import jax.numpy as jnp

def _softmax(x, axis=-1):
    return jax.nn.softmax(x, axis=axis)

def _gelu(x):
    return jax.nn.gelu(x, approximate=True)

def _silu(x):
    return jax.nn.silu(x)

def _sigmoid(x):
    return jax.nn.sigmoid(x)

def _layernorm(x, axis=-1, eps=1e-05):
    m = jnp.mean(x, axis=axis, keepdims=True)
    v = jnp.var(x, axis=axis, keepdims=True)
    return (x - m) / jnp.sqrt(v + eps)

def _scatter_add(tgt, idx, src, axis=0):
    return tgt.at[idx].add(src)

def _segment_sum(src, seg, n):
    return jax.ops.segment_sum(src, seg, n)
kernel_name = 'mk_decoder_preln_d1_seqx_r8_6743ec'

def setup_inputs(seed: int=0):
    np.random.seed(seed)
    _w = jnp.asarray

    def _rec_inputs():
        import jax
        import jax.numpy as jnp
        _rk = jax.random.key(seed)
        x = 0.0003765 + 1 * jax.random.normal(jax.random.fold_in(_rk, 1), (8, 128, 256), jnp.float32)
        _lenS = 128 - jax.random.randint(jax.random.fold_in(_rk, 7), (8,), 0, max(1, 128 // 4) + 1, jnp.int32)
        _lenS2 = 128 - jax.random.randint(jax.random.fold_in(_rk, 8), (8,), 0, max(1, 128 // 4) + 1, jnp.int32)
        _ctx_2048P = jax.random.normal(jax.random.fold_in(_rk, 11), (8, 16, 256), jnp.float32)
        _ctx_2048c = jax.random.dirichlet(jax.random.fold_in(_rk, 511), 0.3 * jnp.ones((16,), jnp.float32), (8, 128))
        _ctx_2048t = jnp.einsum('bsk,bkd->bsd', _ctx_2048c, _ctx_2048P)
        _ctx_2048t = _ctx_2048t * jax.lax.rsqrt(jnp.mean(jnp.square(_ctx_2048t)) + 1e-12) * 0.953939
        ctx_2048 = -0.000292821 + 1.00034 * (_ctx_2048t + 0.3 * jax.random.normal(jax.random.fold_in(_rk, 611), (8, 128, 256), jnp.float32))
        return (x, ctx_2048)
    x, ctx_2048 = _rec_inputs()

    def _L0_attn_setup():
        import jax, jax.numpy as jnp
        import numpy as np
        HEADS = 16
        key = jax.random.key(seed)
        ks = jax.random.split(key, 5)
        B, T, D = (2, 256, 256)
        s = 0.02
        return {'x': jax.random.normal(ks[0], (B, T, D), dtype=jnp.float32), 'Wq': jax.random.normal(ks[1], (D, D), dtype=jnp.float32) * s, 'Wk': jax.random.normal(ks[2], (D, D), dtype=jnp.float32) * s, 'Wv': jax.random.normal(ks[3], (D, D), dtype=jnp.float32) * s, 'Wo': jax.random.normal(ks[4], (D, D), dtype=jnp.float32) * s}
    _L0_attn_all = _L0_attn_setup()
    _L0_attn_in = {k: v for k, v in _L0_attn_all.items() if k in ('Wq', 'Wk', 'Wv', 'Wo')}
    del _L0_attn_all

    def _L0_xattn_setup():
        import jax, jax.numpy as jnp
        import numpy as np
        key = jax.random.key(seed)
        k1, k2, k3, k4, k5 = jax.random.split(key, 5)
        B, D_MODEL, L = (2, 128, 256)
        HEAD_DIM = 8
        H = D_MODEL // HEAD_DIM
        return {'k': jax.random.normal(k1, (B, D_MODEL, L), dtype=jnp.float32), 'v': jax.random.normal(k2, (B, D_MODEL, L), dtype=jnp.float32), 'q': jax.random.normal(k3, (B, D_MODEL, L), dtype=jnp.float32), 'ssm_kernel': jax.random.normal(k4, (H, L), dtype=jnp.float32), 'D': jax.random.normal(k5, (H,), dtype=jnp.float32), 'head_dim': HEAD_DIM}
    _L0_xattn_all = _L0_xattn_setup()
    _L0_xattn_in = {k: v for k, v in _L0_xattn_all.items() if k in ('ssm_kernel', 'D')}
    del _L0_xattn_all

    def _L0_ffn_setup():
        import jax, jax.numpy as jnp
        import numpy as np
        BLOCK_SIZE = 32
        HIDDEN_SIZE = 256
        MLP_DIM = 2048
        NVFP4_LUT = jnp.array([0.0, 0.5, 1.0, 1.5, 2.0, 3.0, 4.0, 6.0, 0.0, -0.5, -1.0, -1.5, -2.0, -3.0, -4.0, -6.0], dtype=jnp.float32)

        def dequant_nvfp4(W_packed, scales, block=BLOCK_SIZE):
            N = W_packed.shape[0]
            low = W_packed & 15
            high = W_packed >> 4 & 15
            idx = jnp.stack([low, high], axis=-1).reshape(N, -1)
            vals = NVFP4_LUT[idx]
            K = vals.shape[1]
            vals = vals.reshape(N, K // block, block) * scales[:, :, None]
            return vals.reshape(N, K)
        key = jax.random.key(seed)
        ks = jax.random.split(key, 7)
        x = jax.random.normal(ks[0], (4, 32, HIDDEN_SIZE), dtype=jnp.float32)
        gate_W_packed = jax.random.randint(ks[1], (MLP_DIM, HIDDEN_SIZE // 2), 0, 32, dtype=jnp.int32)
        gate_scales = jax.random.uniform(ks[2], (MLP_DIM, HIDDEN_SIZE // BLOCK_SIZE), dtype=jnp.float32) * 0.1 + 0.001
        up_W_packed = jax.random.randint(ks[3], (MLP_DIM, HIDDEN_SIZE // 2), 0, 32, dtype=jnp.int32)
        up_scales = jax.random.uniform(ks[4], (MLP_DIM, HIDDEN_SIZE // BLOCK_SIZE), dtype=jnp.float32) * 0.1 + 0.001
        down_W_packed = jax.random.randint(ks[5], (HIDDEN_SIZE, MLP_DIM // 2), 0, 32, dtype=jnp.int32)
        down_scales = jax.random.uniform(ks[6], (HIDDEN_SIZE, MLP_DIM // BLOCK_SIZE), dtype=jnp.float32) * 0.1 + 0.001
        return {'x': x, 'gate_W_packed': gate_W_packed, 'gate_scales': gate_scales, 'up_W_packed': up_W_packed, 'up_scales': up_scales, 'down_W_packed': down_W_packed, 'down_scales': down_scales}
    _L0_ffn_all = _L0_ffn_setup()
    _L0_ffn_in = {k: v for k, v in _L0_ffn_all.items() if k in ('gate_W_packed', 'gate_scales', 'up_W_packed', 'up_scales', 'down_W_packed', 'down_scales')}
    del _L0_ffn_all
    return {'x': x, 'ctx_2048': ctx_2048, 'L0_attn_Wq': _L0_attn_in['Wq'], 'L0_attn_Wk': _L0_attn_in['Wk'], 'L0_attn_Wv': _L0_attn_in['Wv'], 'L0_attn_Wo': _L0_attn_in['Wo'], 'L0_xattn_ssm_kernel': _L0_xattn_in['ssm_kernel'], 'L0_xattn_D': _L0_xattn_in['D'], 'L0_ffn_gate_W_packed': _L0_ffn_in['gate_W_packed'], 'L0_ffn_gate_scales': _L0_ffn_in['gate_scales'], 'L0_ffn_up_W_packed': _L0_ffn_in['up_W_packed'], 'L0_ffn_up_scales': _L0_ffn_in['up_scales'], 'L0_ffn_down_W_packed': _L0_ffn_in['down_W_packed'], 'L0_ffn_down_scales': _L0_ffn_in['down_scales']}

def reference(x, ctx_2048, L0_attn_Wq, L0_attn_Wk, L0_attn_Wv, L0_attn_Wo, L0_xattn_ssm_kernel, L0_xattn_D, L0_ffn_gate_W_packed, L0_ffn_gate_scales, L0_ffn_up_W_packed, L0_ffn_up_scales, L0_ffn_down_W_packed, L0_ffn_down_scales):
    import jax
    import jax.numpy as jnp

    def _L0_attn_ref(x, Wq, Wk, Wv, Wo):
        import jax, jax.numpy as jnp
        import numpy as np
        HEADS = 16
        B, T, _ = x.shape
        H = HEADS
        Dh = Wq.shape[1] // H
        q = (x @ Wq).reshape(B, T, H, Dh)
        k = (x @ Wk).reshape(B, T, H, Dh)
        v = (x @ Wv).reshape(B, T, H, Dh)
        scores = jnp.einsum('bthd,bshd->bhts', q, k)
        mask = jnp.tril(jnp.ones((T, T), dtype=scores.dtype))
        scores = scores * mask
        attn = jax.nn.softmax(scores / T ** 0.5, axis=-1)
        out = jnp.einsum('bhts,bshd->bthd', attn, v).reshape(B, T, H * Dh)
        return out @ Wo

    def _L0_xattn_ref(k, v, q, ssm_kernel, D, head_dim):
        import jax, jax.numpy as jnp
        import numpy as np
        B, HD, L = k.shape
        H = HD // head_dim
        fft_size = 2 * L
        k_ = k.reshape(B, H, head_dim, L)
        v_ = v.reshape(B, H, head_dim, L)
        q_ = q.reshape(B, H, head_dim, L)
        kv = jnp.einsum('bhil,bhjl->bijhl', k_, v_)
        kv_f = jnp.fft.rfft(kv, n=fft_size)
        kernel_f = jnp.fft.rfft(ssm_kernel, n=fft_size)
        y = jnp.fft.irfft(kv_f * kernel_f, n=fft_size)[..., :L]
        out = y + kv * D[None, None, None, :, None]
        out = jnp.einsum('bijhl,bhil->bjhl', out, q_)
        out = jnp.transpose(out, (0, 2, 1, 3)).reshape(B, H * head_dim, L)
        return out.astype(k.dtype)

    def _L0_ffn_ref(x, gate_W_packed, gate_scales, up_W_packed, up_scales, down_W_packed, down_scales):
        import jax, jax.numpy as jnp
        import numpy as np
        BLOCK_SIZE = 32
        HIDDEN_SIZE = 256
        MLP_DIM = 2048
        NVFP4_LUT = jnp.array([0.0, 0.5, 1.0, 1.5, 2.0, 3.0, 4.0, 6.0, 0.0, -0.5, -1.0, -1.5, -2.0, -3.0, -4.0, -6.0], dtype=jnp.float32)

        def dequant_nvfp4(W_packed, scales, block=BLOCK_SIZE):
            N = W_packed.shape[0]
            low = W_packed & 15
            high = W_packed >> 4 & 15
            idx = jnp.stack([low, high], axis=-1).reshape(N, -1)
            vals = NVFP4_LUT[idx]
            K = vals.shape[1]
            vals = vals.reshape(N, K // block, block) * scales[:, :, None]
            return vals.reshape(N, K)
        B, S, H = x.shape
        xt = x.reshape(B * S, H)
        Wg = dequant_nvfp4(gate_W_packed, gate_scales)
        Wu = dequant_nvfp4(up_W_packed, up_scales)
        Wd = dequant_nvfp4(down_W_packed, down_scales)
        gate = jnp.einsum('th,nh->tn', xt, Wg)
        up = jnp.einsum('th,nh->tn', xt, Wu)
        gelu = jnp.tanh(0.7978845608028654 * (gate + 0.044715 * gate ** 3)) * gate * 0.5 + gate * 0.5
        inter = gelu * up
        out = jnp.einsum('tn,hn->th', inter, Wd)
        return out.reshape(B, S, H)
    x = x + _L0_attn_ref(_layernorm(x, axis=-1), L0_attn_Wq, L0_attn_Wk, L0_attn_Wv, L0_attn_Wo)
    x = x + _L0_xattn_ref(ctx_2048, ctx_2048, _layernorm(x, axis=-1), L0_xattn_ssm_kernel, L0_xattn_D, 8)
    x = x + _L0_ffn_ref(_layernorm(x, axis=-1), L0_ffn_gate_W_packed, L0_ffn_gate_scales, L0_ffn_up_W_packed, L0_ffn_up_scales, L0_ffn_down_W_packed, L0_ffn_down_scales)
    return x

_drawn_inputs = setup_inputs


def setup_inputs(seed=0):
    import zlib

    import numpy as np

    out = dict(_drawn_inputs(seed))
    spreads = {}
    factors = {'L0_attn_Wq': 8.0, 'L0_attn_Wk': 8.0, 'L0_attn_Wv': 3.317, 'L0_attn_Wo': 3.328}
    for name, (base, spread) in spreads.items():
        noise = np.random.default_rng([zlib.crc32(name.encode()), seed]).standard_normal(out[name].shape)
        drawn = base * np.exp(spread * noise) if base else spread * noise
        out[name] = jnp.asarray(drawn.astype(out[name].dtype))
    for name, factor in factors.items():
        out[name] = (out[name] * factor).astype(out[name].dtype)
    return out
```

```python
from contextlib import ExitStack

import concourse.bass as bass
from concourse import mybir

F32, F16, BF16, I32 = mybir.dt.float32, mybir.dt.float16, mybir.dt.bfloat16, mybir.dt.int32
ACT = mybir.ActivationFunctionType
ALU = mybir.AluOpType
AX = mybir.AxisListType

P = 128
B = 8
D = 256
NC_ = D // P
H = 16
DH = D // H
HD = 8
NPAIR = 5
NSLOT = 11
MLP = 2048
STEPS = MLP // D
UNITS = STEPS * 4
HALF = 512
EPS = 1e-5
SCALE = 1.0 / 128 ** 0.5
NEG = -1.0e30
W_GAIN = 16.0
DECODE_GAIN = 2.0 ** 14 * W_GAIN
GELU_A, GELU_B = 0.7978845608028654, 0.044715
GATE_K = W_GAIN ** 2 / GELU_B
TANH_SCALE = GELU_A * GELU_B / W_GAIN ** 3
UP_SCALE = 0.5 / W_GAIN ** 2


def build(nc, x_d, ctx_d, wqkv_d, wo_d, ker_d, skip_d, gu_scale_d, down_scale_d, codes_d, out_d):
    scr = nc.dram_tensor("qk_scratch", (2, 2, H, 3, DH, HALF), F16, kind="Internal").ap()

    ctx = ExitStack()
    with ctx:
        def sb(name, shape, dt=F32):
            return ctx.enter_context(nc.sbuf_tensor(name, shape, dt))

        def sem(name):
            return ctx.enter_context(nc.semaphore(name))

        def view(ap, dims, offset=0):
            return bass.AP(ap.tensor, ap.offset + offset, [list(ap.ap[0])] + [list(d) for d in dims])

        X = sb("X", [P, B, D])
        XN = sb("XN", [P, B, D])
        xTh = sb("xTh", [P, NC_, B * P], F16)
        xTl = sb("xTl", [P, NC_, B * P], F16)
        wqkvh = sb("wqkvh", [P, NC_, 3, D], F16)
        wqkvl = sb("wqkvl", [P, NC_, 3, D], F16)
        woh = sb("woh", [P, NC_, D], F16)
        wol = sb("wol", [P, NC_, D], F16)
        Ys = sb("Ys", [P, B, 2 * H, NPAIR * HD])
        early = Ys[:, :, :, :].rearrange("p a b c -> p (a b c)")
        wqkv32 = early[:, 2048:3584].rearrange("p (c w n) -> p c w n", c=NC_, w=3)
        wo32 = early[:, 3584:4096].rearrange("p (c n) -> p c n", c=NC_)
        nat = early[:, 4096:8192].bitcast(F16).rearrange(
            "p (g k m s t) -> p g k m s t", g=2, k=2, m=2, s=2)
        arena = sb("arena", [P, 9728])
        kx = arena[:, 0:3072].rearrange("p (m b h i) -> p m b h i", m=2, b=B, h=H)
        KVR = 4
        KV = arena[:, 3072:5632].rearrange("p (r m n) -> p r m n", r=KVR, m=2)
        T = arena[:, 5632:9728].rearrange("p (h l) -> p h l", h=H)
        Z = arena[:, 0:5632].rearrange("p (r h s) -> p r h s", r=2, h=2 * H)
        codes = arena[:, 5632:7168].bitcast(I32).rearrange("p (r n) -> p r n", r=2)
        scales = arena[:, 7168:8704].rearrange("p (r n) -> p r n", r=2)
        bits = arena[:, 8704:9472].bitcast(I32)
        Wh = sb("Wh", [P, 2, 2, 768], F16)
        Wl = sb("Wl", [P, 2, 2, 768], F16)
        QK = sb("QK", [P, 2, H // 2, B * P], F16)
        late = QK[:, :, :, :].rearrange("p a b c -> p (a b c)").bitcast(F32)
        sq = late[:, 0:1024].rearrange("p (r t) -> p r t", r=2)
        poly = late[:, 1024:2048].rearrange("p (r t) -> p r t", r=2)
        th = late[:, 2048:3072].rearrange("p (r t) -> p r t", r=2)
        gel = late[:, 3072:4096].rearrange("p (r t) -> p r t", r=2)
        act = late[:, 4096:5120].rearrange("p (r t) -> p r t", r=2)
        IR = 4
        ih = late[:, 5120:6144].bitcast(F16).rearrange("p (r t) -> p r t", r=IR)
        il = late[:, 6144:7168].bitcast(F16).rearrange("p (r t) -> p r t", r=IR)
        bits2 = late[:, 7168:7936].bitcast(I32)
        vaug = sb("vaug", [P, B, H, 32])
        PR = 4
        PT = sb("PT", [P, PR, 4, P])
        W32 = PT[:, 0:3, :, :].rearrange("p a b c -> p (a b c)").rearrange("p (n w) -> p n w", n=2)
        pvs = sb("pvs", [P, 2, 512])
        tail = sb("tail", [P, H, DH + 1])
        num = sb("num", [P, H, DH + 1])
        rec = sb("rec", [P, H])
        o_sb = sb("o_sb", [P, 2, D])
        oTh = sb("oTh", [P, 2, NC_, P], F16)
        oTl = sb("oTl", [P, 2, NC_, P], F16)
        qx = sb("qx", [P, 2, 2 * H, 12])
        R = sb("R", [P, 2, 2 * H, HD])
        stats = sb("stats", [P, B, 6])
        mv = sb("mv", [P, B, 2])
        veps = sb("veps", [P, B])
        rstd = sb("rstd", [P, B])
        nhalf = sb("nhalf", [P, B])
        mx = sb("mx", [P, 2, H])
        mm = sb("mm", [P, 2, H])
        res1 = sb("res1", [P, H])
        res2 = sb("res2", [P, H])
        mp = sb("mp", [P, 2, 112], BF16)
        mT = sb("mT", [112, 2, P], BF16)
        em = sb("em", [P, 2, H])
        ident = sb("ident", [P, P])
        anti = sb("anti", [P, P])
        identb = sb("identb", [P, P], BF16)
        later = sb("later", [P, P])
        maskb = sb("maskb", [P, 4, P], BF16)
        sel = sb("sel", [112, H, P], BF16)
        guard = sb("guard", [P, 1])
        skip = sb("skip", [P, H])

        bank = [ctx.enter_context(nc.psum_tensor(f"bank{i}", [P, 512], F32)) for i in range(8)]

        s_x = [sem(f"s_xin{g}") for g in range(2)]
        s_wqkv, s_wo, s_skip = sem("s_wqkv"), sem("s_wo"), sem("s_skip")
        s_ctx = [sem(f"s_ctx{g}") for g in range(2)]
        s_toep = [sem(f"s_toep{g}") for g in range(2)]
        s_const = sem("s_const")
        s_zero = sem("s_zero")
        s_st = sem("s_st")
        s_mv = sem("s_mv")
        s_ve = sem("s_ve")
        s_rstd = sem("s_rstd")
        s_xn = sem("s_xn")
        s_xt = sem("s_xt")
        s_xth, s_xtl = sem("s_xth"), sem("s_xtl")
        s_wh, s_wl = sem("s_wh"), sem("s_wl")
        s_qk = sem("s_qk")
        s_qkh, s_qkl = sem("s_qkh"), sem("s_qkl")
        s_scr = [sem(f"s_scr{i}") for i in range(4)]
        s_pack = [[sem(f"s_pack{g}{k}") for k in range(2)] for g in range(2)]
        s_v, s_vs = sem("s_v"), sem("s_vs")
        s_tdiag = sem("s_tdiag")
        s_kv = [sem("s_kv0"), sem("s_kv1")]
        s_y, s_ys = sem("s_y"), sem("s_ys")
        s_s, s_max = sem("s_s"), sem("s_max")
        s_mch = sem("s_mch")
        s_em = sem("s_em")
        s_mpt = sem("s_mpt")
        s_mt = sem("s_mt")
        s_stt = sem("s_stt")
        s_exp, s_msk, s_pv = sem("s_exp"), sem("s_msk"), sem("s_pv")
        s_pvs, s_tok, s_suf = sem("s_pvs"), sem("s_tok"), sem("s_suf")
        s_och = sem("s_och")
        s_ot, s_oth, s_otl, s_proj, s_x1 = sem("s_ot"), sem("s_oth"), sem("s_otl"), sem("s_proj"), sem("s_x1")
        s_qt, s_qx, s_z, s_r = sem("s_qt"), sem("s_qx"), sem("s_z"), sem("s_r")
        s_rt, s_x2 = sem("s_rt"), sem("s_x2")
        s_yt, s_yth, s_ytl = sem("s_yt"), sem("s_yth"), sem("s_ytl")
        s_code = [sem(f"s_code{r}") for r in range(2)]
        s_bits = sem("s_bits")
        s_w32, s_ffh, s_ffl = sem("s_w32"), sem("s_ffh"), sem("s_ffl")
        s_g, s_u, s_sq, s_poly, s_th = sem("s_g"), sem("s_u"), sem("s_sq"), sem("s_poly"), sem("s_th")
        s_gel, s_act, s_ih, s_il, s_down = sem("s_gel"), sem("s_act"), sem("s_ih"), sem("s_il"), sem("s_down")
        s_fin, s_out = sem("s_fin"), sem("s_out")
        block = ctx.enter_context(nc.Block())

        SLOTS = B + 4
        ln_order = [("ln1", b) for b in range(B)]
        for s in range(SLOTS):
            if 0 <= s - 4 < B:
                ln_order.append(("ln3", s - 4))
            if 0 <= s - 2 < B:
                ln_order.append(("ln2", s - 2))
        ln_count = {which: n + 1 for n, which in enumerate(ln_order)}

        def head_group(g):
            return g % 2, [4 * (g // 2) + j for j in range(4)]

        @block.sync
        def _(sp):
            for g in range(2):
                sp.dma_start(X[:, 4 * g:4 * g + 4, :],
                             x_d[4 * g:4 * g + 4].rearrange("b t d -> t b d")).then_inc(s_x[g], 16)
                if g == 0:
                    for w in range(3):
                        sp.dma_start(wqkv32[:, :, w, :],
                                     wqkv_d[w].rearrange("(c p) n -> p c n", p=P)).then_inc(s_wqkv, 16)
            for m in range(2):
                sp.dma_start(kx[:, m], ctx_d[m]).then_inc(s_ctx[m], 16)
            sp.dma_start(skip[:, :], bass.AP(skip_d.tensor, skip_d.offset, [[0, P], [1, H]])).then_inc(s_skip, 16)
            for g in range(2):
                sp.dma_start(T[:, 8 * g:8 * g + 8, :],
                             bass.AP(ker_d.tensor, ker_d.offset + 1 + 8 * g * 384,
                                     [[1, P], [384, 8], [1, D]])).then_inc(s_toep[g], 16)
            sp.dma_start(wo32, wo_d.rearrange("(c p) n -> p c n", p=P)).then_inc(s_wo, 16)
            for g in range(2):
                for k in range(2):
                    sp.wait_ge(s_qkl, 4 * g + 2 * k + 2)
                    for m in range(2):
                        for part in range(3 if k == 0 else 2):
                            sp.dma_start(scr[g, k, 8 * m:8 * m + 8, part],
                                         nat[:, g, k, m, part % 2, :]).then_inc(s_scr[2 * g + k], 16)
                for k in range(2):
                    sp.wait_ge(s_scr[2 * g + k], 96 if k == 0 else 64)
                    for par in range(2):
                        for two in range(2):
                            first = 1 if k == 0 and two else 0
                            src = scr[g, k, par::2, first:first + 2].rearrange("h s d t -> (s d) h t")
                            rows = 64 * par + 32 * two
                            sp.dma_start(QK[rows:rows + 32, k, :, HALF * g:HALF * g + HALF],
                                         src).then_inc(s_pack[g][k], 16)

            def load_codes(j):
                r = j % 2
                if j == 0:
                    sp.wait_ge(s_y, 2 * H)
                if j >= 2:
                    sp.wait_ge(s_w32, j - 1)
                sp.dma_start(codes[:, r, :], codes_d[j]).then_inc(s_code[r], 16)
                sp.dma_start(scales[:, r, 0:512], bass.AP(
                    gu_scale_d.tensor, gu_scale_d.offset + j * 8 * 512,
                    [[512, 8], [0, 16], [1, 512]])).then_inc(s_code[r], 16)
                sp.dma_start(scales[:, r, 512:768], bass.AP(
                    down_scale_d.tensor, down_scale_d.offset + j * 8 * D,
                    [[D, 8], [0, 16], [1, D]])).then_inc(s_code[r], 16)

            for j in range(STEPS):
                load_codes(j)
            for b in range(B):
                sp.wait_ge(s_fin, b + 1)
                sp.dma_start(out_d[b], XN[:, b, :]).then_inc(s_out, 16)
            sp.wait_ge(s_out, 16 * B)

        @block.gpsimd
        def _(pool):
            g_ = nc.gpsimd
            z = [0]

            def own(ins):
                z[0] += 1
                ins.then_inc(s_zero, 1)
                pool.wait_ge(s_zero, z[0])

            own(g_.memset(ident[:, :], 0.0))
            g_.affine_select(out=ident[:, :], in_=ident[:, :], compare_op=ALU.not_equal, fill=1.0, base=0,
                             pattern=[[-1, P]], channel_multiplier=1).then_inc(s_const, 1)
            own(g_.memset(anti[:, :], 0.0))
            g_.affine_select(out=anti[:, :], in_=anti[:, :], compare_op=ALU.not_equal, fill=1.0,
                             base=-(P - 1), pattern=[[1, P]], channel_multiplier=1).then_inc(s_const, 1)
            own(g_.memset(nhalf[:, :], -0.5))

            def rstds(n0, n):
                own(g_.tensor_scalar(veps[:, n0:n0 + n], mv[:, n0:n0 + n, 1], EPS, None, ALU.add))
                g_.tensor_tensor(rstd[:, n0:n0 + n], veps[:, n0:n0 + n], nhalf[:, n0:n0 + n],
                                 ALU.pow).then_inc(s_rstd, n)

            for g in range(2):
                pool.wait_ge(s_mv, 4 * g + 4)
                rstds(4 * g, 4)
                if g == 0:
                    g_.memset(vaug[:, :, :, DH:DH + 1], 1.0).then_inc(s_const, 1)
                    g_.memset(vaug[:, :, :, DH + 1:32], 0.0).then_inc(s_const, 1)
            own(g_.memset(maskb[:, :, :], 0.0))
            g_.affine_select(out=maskb[:, :, :], in_=maskb[:, :, :], compare_op=ALU.is_ge, fill=NEG, base=0,
                             pattern=[[0, 4], [-1, P]], channel_multiplier=1).then_inc(s_const, 1)
            own(g_.memset(later[:, :], 1.0))
            g_.affine_select(out=later[:, :], in_=later[:, :], compare_op=ALU.is_gt, fill=0.0, base=0,
                             pattern=[[-1, P]], channel_multiplier=1).then_inc(s_const, 1)
            own(g_.memset(identb[:, :], 0.0))
            g_.affine_select(out=identb[:, :], in_=identb[:, :], compare_op=ALU.not_equal, fill=1.0, base=0,
                             pattern=[[-1, P]], channel_multiplier=1).then_inc(s_const, 1)
            own(g_.memset(guard[:, :], 0.0))
            g_.affine_select(out=guard[:, :], in_=guard[:, :], compare_op=ALU.not_equal, fill=NEG,
                             base=-(P - 1), pattern=[[0, 1]], channel_multiplier=1).then_inc(s_const, 1)
            own(g_.memset(sel[:, :, :], 0.0))
            for n, first in enumerate([0, 16, 32, 64, 80, 96]):
                own(g_.affine_select(out=sel[:, :, :], in_=sel[:, :, :], compare_op=ALU.not_equal, fill=-1.0,
                                     base=-first, pattern=[[-1, H], [0, P]], channel_multiplier=1))
            g_.memset(mp[:, :, 48:64], 0.0).then_inc(s_const, 1)

            def products(h):
                m = 1
                if h >= KVR:
                    pool.wait_ge(s_y, 2 * (h - KVR) + 2)
                a = kx[:, m, :, h, :]
                g_.tensor_tensor(
                    view(KV[:, h % KVR, m, :], [[40, B], [8, NPAIR], [1, HD]]),
                    view(a, [[12 * H, B], [0, NPAIR], [1, HD]]),
                    view(a, [[12 * H, B], [1, NPAIR], [1, HD]]), ALU.mult).then_inc(s_kv[1], 1)

            pool.wait_ge(s_ctx[1], 16)
            for h in range(H):
                products(h)

            def mask(b, g):
                n = 4 * b + g
                pool.wait_ge(s_exp, n + 1)
                g_.affine_select(out=PT[:, n % PR], in_=PT[:, n % PR], compare_op=ALU.is_ge, fill=0.0, base=0,
                                 pattern=[[0, 4], [1, P]], channel_multiplier=-1).then_inc(s_msk, 1)

            def conv_products(b):
                r = b % 2
                pool.wait_ge(s_qx, b + 1)
                pool.wait_ge(s_ys, 2 * H)
                if b >= 2:
                    pool.wait_ge(s_r, b - 1)
                g_.tensor_tensor(view(Z[:, r], [[88, 2 * H], [8, NPAIR], [1, HD]]),
                                 view(Ys[:, b], [[40, 2 * H], [8, NPAIR], [1, HD]]),
                                 view(qx[:, r], [[12, 2 * H], [1, NPAIR], [1, HD]]), ALU.mult).then_inc(s_z, 1)
                g_.tensor_tensor(view(Z[:, r], [[88, 2 * H], [17, 3], [1, HD]], 41),
                                 view(Ys[:, b], [[40, 2 * H], [8, 3], [1, HD]], 8),
                                 view(qx[:, r], [[12, 2 * H], [0, 3], [1, HD]]), ALU.mult).then_inc(s_z, 1)

            def decode_scale(j):
                pool.wait_ge(s_bits, 4 * j + 4)
                pool.wait_ge(s_code[j % 2], 48 * (j // 2 + 1))
                if j == 0:
                    pool.wait_ge(s_pv, 4 * B)
                else:
                    pool.wait_ge(s_ffl, j)
                g_.tensor_tensor(W32[:, :, :],
                                 view(bits[:, :].bitcast(F16), [[1, 2], [2, 768]]),
                                 view(scales[:, j % 2, :], [[0, 2], [1, 768]]), ALU.mult).then_inc(s_w32, 1)

            pool.wait_ge(s_y, 2 * H)
            own(g_.memset(Z, 0.0))
            for s in range(SLOTS):
                b4, b3, b2, b1 = s - 4, s - 3, s - 2, s - 1
                if 0 <= b3 < B:
                    conv_products(b3)
                if 0 <= b1 < B:
                    mask(b1, 0)
                    mask(b1, 1)
                if 0 <= b4 < B:
                    pool.wait_ge(s_mv, ln_count["ln3", b4])
                    rstds(b4, 1)
                if 0 <= b1 < B:
                    mask(b1, 2)
                if 0 <= b2 < B:
                    pool.wait_ge(s_mv, ln_count["ln2", b2])
                    rstds(b2, 1)
                if 0 <= b1 < B:
                    mask(b1, 3)
                if s == SLOTS - 2:
                    decode_scale(0)
            for u in range(UNITS):
                if u % 4 == 1 and u // 4 + 1 < STEPS:
                    decode_scale(u // 4 + 1)
                pool.wait_ge(s_ih, u + 1)
                if u >= IR:
                    pool.wait_ge(s_down, u - IR + 1)
                g_.tensor_tensor(il[:, u % IR], act[:, u % 2], ih[:, u % IR], ALU.subtract).then_inc(s_il, 1)

        @block.scalar
        def _(sc):
            s_ = nc.scalar
            sc.wait_ge(s_wqkv, 48)
            s_.activation(wqkvh[:, :, :, :], wqkv32, ACT.Copy).then_inc(s_wh, 1)
            for g in range(2):
                for pr in range(2 * g, 2 * g + 2):
                    sc.wait_ge(s_xt, pr + 1)
                    s_.activation(xTh[:, :, 256 * pr:256 * pr + 256].rearrange("p c (b t) -> p b c t", b=2),
                                  bank[pr % 2][:, :].rearrange("p (b c t) -> p b c t", b=2, c=2),
                                  ACT.Copy).then_inc(s_xth, 1)
                if g == 0:
                    sc.wait_ge(s_wo, 16)
                    s_.activation(woh[:, :, :], wo32, ACT.Copy).then_inc(s_wh, 1)
            def q_hi(g):
                for n in range(4):
                    sc.wait_ge(s_qk, 4 * g + n + 1)
                    s_.activation(nat[:, g, n // 2, n % 2, 0, :], bank[2 + n][:, :],
                                  ACT.Copy).then_inc(s_qkh, 1)

            def v_out(g):
                for b in range(4 * g, 4 * g + 4):
                    sc.wait_ge(s_v, b + 1)
                    s_.activation(vaug[:, b, :, 0:DH],
                                  bank[6 + b % 2][:, 0:D].rearrange("p (h d) -> p h d", h=H),
                                  ACT.Copy).then_inc(s_vs, 1)

            for g in range(2):
                q_hi(g)
                v_out(g)
            sc.wait_ge(s_wl, 2)
            for g in range(2):
                for k in range(2):
                    sc.wait_ge(s_scr[2 * g + k], 96 if k == 0 else 64)
            for h in range(H):
                for lc in range(2):
                    n = 2 * h + lc
                    sc.wait_ge(s_y, n + 1)
                    s_.activation(Ys[:, :, lc * H + h, :],
                                  bank[2 + n % 4][:, 0:320].rearrange("p (b k) -> p b k", b=B),
                                  ACT.Copy).then_inc(s_ys, 1)

            def exp_max(b):
                sc.wait_ge(s_mch, 5 * b + 1)
                if b >= 2:
                    sc.wait_ge(s_och, 4 * (b - 2) + 1)
                s_.activation(em[:, b % 2, :], mm[:, b % 2, :], ACT.Exp, scale=-SCALE).then_inc(s_em, 1)

            def probs(b, g):
                n = 4 * b + g
                sc.wait_ge(s_stt, n + 1)
                if n >= PR:
                    sc.wait_ge(s_pv, n - PR + 1)
                s_.activation(PT[:, n % PR].rearrange("p a b -> p (a b)"), bank[2 + n % 2][:, :],
                              ACT.Exp, scale=SCALE).then_inc(s_exp, 1)

            def pv_out(b):
                sc.wait_ge(s_pv, 4 * b + 4)
                if b >= 2:
                    sc.wait_ge(s_tok, b - 1)
                s_.activation(pvs[:, b % 2, :], bank[4][:, :], ACT.Copy).then_inc(s_pvs, 1)

            for s in range(SLOTS):
                b4, b3, b2, b1, b0 = s - 4, s - 3, s - 2, s - 1, s
                if 0 <= b3 < B:
                    sc.wait_ge(s_qt, b3 + 1)
                    if b3 >= 2:
                        sc.wait_ge(s_z, 2 * (b3 - 2) + 2)
                    r = b3 % 2
                    s_.activation(qx[:, r, :, 8:12], view(bank[7][:, :], [[8, 2 * H], [1, 4]]),
                                  ACT.Copy)
                    s_.activation(qx[:, r, :, 0:8], view(bank[7][:, :], [[8, 2 * H], [1, 8]]),
                                  ACT.Copy).then_inc(s_qx, 1)
                if 0 <= b1 < B:
                    probs(b1, 0)
                    probs(b1, 1)
                if 0 <= b2 < B:
                    sc.wait_ge(s_ot, b2 + 1)
                    if b2 >= 2:
                        sc.wait_ge(s_proj, b2 - 1)
                    s_.activation(oTh[:, b2 % 2], bank[7][:, 0:D].rearrange("p (c t) -> p c t", c=2),
                                  ACT.Copy).then_inc(s_oth, 1)
                if 0 <= b1 < B:
                    probs(b1, 2)
                if 0 <= b4 < B:
                    sc.wait_ge(s_yt, b4 + 1)
                    s_.activation(xTh[:, :, P * b4:P * b4 + P],
                                  bank[7][:, 0:D].rearrange("p (c t) -> p c t", c=2),
                                  ACT.Copy).then_inc(s_yth, 1)
                if 0 <= b1 < B:
                    probs(b1, 3)
                if b0 < B:
                    exp_max(b0)
                    sc.wait_ge(s_mpt, b0 + 1)
                    if b0 >= 2:
                        sc.wait_ge(s_stt, 4 * (b0 - 2) + 4)
                    s_.activation(mT[:, b0 % 2, :], bank[7][:, 0:64].bitcast(BF16)[0:112, :],
                                  ACT.Copy).then_inc(s_mt, 1)
                if 0 <= b1 < B:
                    pv_out(b1)

                if s == SLOTS - 2:
                    sc.wait_ge(s_w32, 1)
                    s_.activation(Wh[:, 0], W32[:, :, :], ACT.Copy, scale=DECODE_GAIN).then_inc(s_ffh, 1)

            def w_hi_step(j):
                sc.wait_ge(s_w32, j + 1)
                if j >= 2:
                    sc.wait_ge(s_down, 4 * (j - 2) + 4)
                s_.activation(Wh[:, j % 2], W32[:, :, :], ACT.Copy, scale=DECODE_GAIN).then_inc(s_ffh, 1)

            def act_hi(u):
                sc.wait_ge(s_act, u + 1)
                if u >= IR:
                    sc.wait_ge(s_down, u - IR + 1)
                s_.activation(ih[:, u % IR], act[:, u % 2], ACT.Copy).then_inc(s_ih, 1)

            for u in range(UNITS):
                sc.wait_ge(s_g, u + 1)
                if u >= 2:
                    sc.wait_ge(s_poly, u - 1)
                s_.activation(sq[:, u % 2], bank[2 * (u % 2)][:, :], ACT.Square).then_inc(s_sq, 1)
                if u >= 1:
                    act_hi(u - 1)
                sc.wait_ge(s_poly, u + 1)
                if u >= 2:
                    sc.wait_ge(s_gel, u - 1)
                s_.activation(th[:, u % 2], poly[:, u % 2], ACT.Tanh, scale=TANH_SCALE).then_inc(s_th, 1)
                if u % 4 == 2 and u // 4 + 1 < STEPS:
                    w_hi_step(u // 4 + 1)
            act_hi(UNITS - 1)

        @block.vector
        def _(ve):
            v_ = nc.vector
            lnc = [0]

            def ln_stats(b):
                lnc[0] += 1
                v_.bn_stats(out=stats[:, b, :], in_=X[:, b, :]).then_inc(s_st, 1)
                ve.wait_ge(s_st, lnc[0])
                v_.bn_aggr(out=mv[:, b, :], in_=stats[:, b, :]).then_inc(s_mv, 1)

            def ln_apply(b, n):
                ve.wait_ge(s_rstd, n)
                v_.tensor_scalar(XN[:, b, :], X[:, b, :], mv[:, b, 0:1], rstd[:, b:b + 1],
                                 ALU.subtract, ALU.mult).then_inc(s_xn, 1)

            def x_lo(pr):
                ve.wait_ge(s_xth, pr + 1)
                v_.tensor_tensor(xTl[:, :, 256 * pr:256 * pr + 256].rearrange("p c (b t) -> p b c t", b=2),
                                 bank[pr % 2][:, :].rearrange("p (b c t) -> p b c t", b=2, c=2),
                                 xTh[:, :, 256 * pr:256 * pr + 256].rearrange("p c (b t) -> p b c t", b=2),
                                 ALU.subtract).then_inc(s_xtl, 1)

            ve.wait_ge(s_x[0], 16)
            for b in range(4):
                ln_stats(b)
            ve.wait_ge(s_wh, 1)
            v_.tensor_tensor(wqkvl[:, :, :, :], wqkv32, wqkvh[:, :, :, :], ALU.subtract).then_inc(s_wl, 1)
            ve.wait_ge(s_x[1], 16)
            for b in range(4, 8):
                ln_stats(b)
            for g in range(2):
                for b in range(4 * g, 4 * g + 4):
                    ln_apply(b, 4 * g + 4)
                for pr in range(2 * g, 2 * g + 2):
                    x_lo(pr)
            ve.wait_ge(s_wh, 2)
            v_.tensor_tensor(wol[:, :, :], wo32, woh[:, :, :], ALU.subtract).then_inc(s_wl, 1)

            def q_lo(g):
                for n in range(4):
                    ve.wait_ge(s_qkh, 4 * g + n + 1)
                    v_.tensor_tensor(nat[:, g, n // 2, n % 2, 1, :], bank[2 + n][:, :],
                                     nat[:, g, n // 2, n % 2, 0, :], ALU.subtract).then_inc(s_qkl, 1)

            q_lo(0)
            q_lo(1)
            ve.wait_ge(s_skip, 16)
            ve.wait_ge(s_const, 2)
            ve.wait_ge(s_toep[0], 16)
            ve.wait_ge(s_toep[1], 16)
            for h in range(H):
                v_.scalar_tensor_tensor(out=T[:, h, 0:P], in0=anti[:, :], scalar=skip[:, h:h + 1],
                                        in1=T[:, h, 0:P], op0=ALU.mult, op1=ALU.add).then_inc(s_tdiag, 1)
            for h in range(H):
                if h == 0:
                    ve.wait_ge(s_ctx[0], 16)
                if h >= KVR:
                    ve.wait_ge(s_y, 2 * (h - KVR) + 2)
                a = kx[:, 0, :, h, :]
                v_.tensor_tensor(view(KV[:, h % KVR, 0, :], [[40, B], [8, NPAIR], [1, HD]]),
                                 view(a, [[12 * H, B], [0, NPAIR], [1, HD]]),
                                 view(a, [[12 * H, B], [1, NPAIR], [1, HD]]), ALU.mult).then_inc(s_kv[0], 1)

            def group_max(b, g):
                n = 4 * b + g
                ve.wait_ge(s_s, n + 1)
                v_.tensor_reduce(mx[:, b % 2, 4 * g:4 * g + 4],
                                 bank[n % 2][:, :].rearrange("p (h t) -> p h t", h=4),
                                 AX.X, ALU.max).then_inc(s_max, 1)

            def split_max(b):
                r = b % 2
                ve.wait_ge(s_max, 4 * b + 4)
                if b == 0:
                    ve.wait_ge(s_const, 9)
                if b >= 2:
                    ve.wait_ge(s_em, b - 1)
                v_.tensor_scalar(mm[:, r, :], mx[:, r, :], guard[:, 0:1], None, ALU.max).then_inc(s_mch, 1)
                ve.wait_ge(s_mch, 5 * b + 1)
                if b >= 2:
                    ve.wait_ge(s_mpt, b - 1)

                def twice(part):
                    return view(mp[:, r, :], [[64, 2], [1, H]], 16 * part)

                def rep(t):
                    return view(t, [[0, 2], [1, H]])

                v_.tensor_copy(twice(0), rep(mm[:, r, :])).then_inc(s_mch, 1)
                ve.wait_ge(s_mch, 5 * b + 2)
                v_.tensor_tensor(res1[:, :], mm[:, r, :], mp[:, r, 0:16], ALU.subtract).then_inc(s_mch, 1)
                ve.wait_ge(s_mch, 5 * b + 3)
                v_.tensor_copy(twice(1), rep(res1[:, :])).then_inc(s_mch, 1)
                ve.wait_ge(s_mch, 5 * b + 4)
                v_.tensor_tensor(twice(2), rep(res1[:, :]), rep(mp[:, r, 16:32]),
                                 ALU.subtract).then_inc(s_mch, 1)

            def normalise(b):
                ve.wait_ge(s_suf, b + 1)
                ve.wait_ge(s_em, b + 1)
                v_.tensor_tensor(tail[:, :, :], bank[6][:, 0:272].rearrange("p (h d) -> p h d", h=H),
                                 view(em[:, b % 2, :], [[1, H], [0, DH + 1]]), ALU.mult).then_inc(s_och, 1)
                ve.wait_ge(s_och, 4 * b + 1)
                ve.wait_ge(s_tok, b + 1)
                v_.tensor_tensor(num[:, :, :], tail[:, :, :], view(bank[5][:, :], [[32, H], [1, DH + 1]]),
                                 ALU.add).then_inc(s_och, 1)
                ve.wait_ge(s_och, 4 * b + 2)
                v_.reciprocal(rec[:, :], num[:, :, DH]).then_inc(s_och, 1)
                ve.wait_ge(s_och, 4 * b + 3)
                v_.tensor_tensor(o_sb[:, b % 2, :].rearrange("p (h d) -> p h d", h=H), num[:, :, 0:DH],
                                 view(rec[:, :], [[1, H], [0, DH]]), ALU.mult).then_inc(s_och, 1)

            def codes_bits(j):
                r = j % 2
                ve.wait_ge(s_code[r], 48 * (j // 2 + 1))
                if j == 0:
                    ve.wait_ge(s_stt, 4 * B)
                v_.scalar_tensor_tensor(out=bits2[:, :], in0=codes[:, r, :], scalar=12, in1=codes[:, r, :],
                                        op0=ALU.logical_shift_left, op1=ALU.bitwise_or).then_inc(s_bits, 1)
                ve.wait_ge(s_bits, 4 * j + 1)
                if j >= 1:
                    ve.wait_ge(s_w32, j)
                v_.tensor_scalar(codes[:, r, :], bits2[:, :], 0x00070007, 9, ALU.bitwise_and,
                                 ALU.logical_shift_left).then_inc(s_bits, 1)
                v_.tensor_scalar(bits[:, :], bits2[:, :], 0x00080008, 12, ALU.bitwise_and,
                                 ALU.logical_shift_left).then_inc(s_bits, 1)
                ve.wait_ge(s_bits, 4 * j + 3)
                v_.tensor_tensor(bits[:, :], bits[:, :], codes[:, r, :], ALU.bitwise_or).then_inc(s_bits, 1)

            def w_lo(j):
                ve.wait_ge(s_ffh, j + 1)
                v_.scalar_tensor_tensor(out=Wl[:, j % 2].rearrange("p a b -> p (a b)"),
                                        in0=W32[:, :, :].rearrange("p a b -> p (a b)"), scalar=DECODE_GAIN,
                                        in1=Wh[:, j % 2].rearrange("p a b -> p (a b)"),
                                        op0=ALU.mult, op1=ALU.subtract).then_inc(s_ffl, 1)

            xn = [B]
            for s in range(SLOTS):
                b4, b3, b2, b1, b0 = s - 4, s - 3, s - 2, s - 1, s
                if b0 < B:
                    group_max(b0, 0)
                    group_max(b0, 1)
                if 0 <= b4 < B:
                    ve.wait_ge(s_rt, b4 + 1)
                    v_.tensor_tensor(X[:, b4, :], X[:, b4, :], bank[7][:, 0:D], ALU.add).then_inc(s_x2, 1)
                    ve.wait_ge(s_x2, b4 + 1)
                    ln_stats(b4)
                if 0 <= b2 < B:
                    normalise(b2)
                if b0 < B:
                    group_max(b0, 2)
                if 0 <= b4 < B:
                    ln_apply(b4, ln_count["ln3", b4])
                if 0 <= b2 < B:
                    ve.wait_ge(s_oth, b2 + 1)
                    v_.tensor_tensor(oTl[:, b2 % 2], bank[7][:, 0:D].rearrange("p (c t) -> p c t", c=2),
                                     oTh[:, b2 % 2], ALU.subtract).then_inc(s_otl, 1)
                if b0 < B:
                    group_max(b0, 3)
                if 0 <= b2 < B:
                    ve.wait_ge(s_proj, b2 + 1)
                    v_.tensor_tensor(X[:, b2, :], X[:, b2, :], bank[6][:, 0:D], ALU.add).then_inc(s_x1, 1)
                    ve.wait_ge(s_x1, b2 + 1)
                    ln_stats(b2)
                if b0 < B:
                    split_max(b0)
                if 0 <= b4 < B:
                    ve.wait_ge(s_yth, b4 + 1)
                    v_.tensor_tensor(xTl[:, :, P * b4:P * b4 + P],
                                     bank[7][:, 0:D].rearrange("p (c t) -> p c t", c=2),
                                     xTh[:, :, P * b4:P * b4 + P], ALU.subtract).then_inc(s_ytl, 1)
                if 0 <= b2 < B:
                    ln_apply(b2, ln_count["ln2", b2])
                if 0 <= b3 < B:
                    ve.wait_ge(s_z, 2 * b3 + 2)
                    if b3 >= 2:
                        ve.wait_ge(s_rt, b3 - 1)
                    v_.tensor_reduce(R[:, b3 % 2], view(Z[:, b3 % 2], [[88, 2 * H], [1, HD], [8, NSLOT]]),
                                     AX.X, ALU.add).then_inc(s_r, 1)
                if s == SLOTS - 3:
                    codes_bits(0)
                if s == SLOTS - 1:
                    w_lo(0)

            def poly_step(u):
                ve.wait_ge(s_sq, u + 1)
                if u >= 2:
                    ve.wait_ge(s_th, u - 1)
                v_.scalar_tensor_tensor(out=poly[:, u % 2], in0=sq[:, u % 2], scalar=GATE_K,
                                        in1=bank[2 * (u % 2)][:, :], op0=ALU.add, op1=ALU.mult).then_inc(s_poly, 1)

            def gate_up(u):
                ve.wait_ge(s_th, u + 1)
                v_.scalar_tensor_tensor(out=gel[:, u % 2], in0=th[:, u % 2], scalar=1.0,
                                        in1=bank[2 * (u % 2)][:, :], op0=ALU.add, op1=ALU.mult).then_inc(s_gel, 1)
                ve.wait_ge(s_gel, u + 1)
                ve.wait_ge(s_u, u + 1)
                if u >= 2:
                    ve.wait_ge(s_il, u - 1)
                v_.scalar_tensor_tensor(out=act[:, u % 2], in0=bank[2 * (u % 2) + 1][:, :], scalar=UP_SCALE,
                                        in1=gel[:, u % 2], op0=ALU.mult, op1=ALU.mult).then_inc(s_act, 1)

            for u in range(UNITS):
                poly_step(u)
                j = u // 4 + 1
                if u % 4 == 0 and j < STEPS:
                    codes_bits(j)
                if u % 4 == 3 and j < STEPS:
                    w_lo(j)
                gate_up(u)
            for b in range(B):
                if b == 0:
                    ve.wait_ge(s_down, UNITS)
                v_.scalar_tensor_tensor(out=XN[:, b, :], in0=bank[4 + b // 2][:, D * (b % 2):D * (b % 2) + D],
                                        scalar=1.0 / W_GAIN, in1=X[:, b, :],
                                        op0=ALU.mult, op1=ALU.add).then_inc(s_fin, 1)

        @block.tensor
        def _(pe):
            t_ = nc.tensor
            mmul = t_.matmul
            pe.wait_ge(s_const, 1)
            for pr in range(4):
                for b in (2 * pr, 2 * pr + 1):
                    pe.wait_ge(s_xn, b + 1)
                    if pr >= 2 and b % 2 == 0:
                        pe.wait_ge(s_xtl, pr - 1)
                    for c in range(2):
                        last = t_.transpose(bank[pr % 2][:, 256 * (b % 2) + P * c:256 * (b % 2) + P * c + P],
                                            XN[:, b, P * c:P * c + P], ident[:, :])
                last.then_inc(s_xt, 1)

            def three(out, ah, al, bh, bl, chunks, **kw):
                n = 0
                for c in chunks:
                    for a, w in ((ah, bh), (ah, bl), (al, bh)):
                        ins = mmul(out, a(c), w(c), start=(n == 0), stop=(n == 3 * len(chunks) - 1))
                        n += 1
                return ins

            def project_qk(g):
                pe.wait_ge(s_xtl, 2 * g + 2)
                pe.wait_ge(s_wl, 1)
                for n in range(4):
                    if g:
                        pe.wait_ge(s_qkl, n + 1)
                    k, m = n // 2, n % 2
                    three(bank[2 + n][:, :],
                          lambda c: wqkvh[:, c, k, P * m:P * m + P], lambda c: wqkvl[:, c, k, P * m:P * m + P],
                          lambda c: xTh[:, c, HALF * g:HALF * g + HALF], lambda c: xTl[:, c, HALF * g:HALF * g + HALF],
                          range(2)).then_inc(s_qk, 1)

            def project_v(g):
                for b in range(4 * g, 4 * g + 4):
                    if b >= 2:
                        pe.wait_ge(s_vs, b - 1)
                    three(bank[6 + b % 2][:, 0:D],
                          lambda c: xTh[:, c, P * b:P * b + P], lambda c: xTl[:, c, P * b:P * b + P],
                          lambda c: wqkvh[:, c, 2, :], lambda c: wqkvl[:, c, 2, :], range(2)).then_inc(s_v, 1)

            for g in range(2):
                project_qk(g)
                project_v(g)
            pe.wait_ge(s_qkl, 8)
            for h in range(H):
                pe.wait_ge(s_tdiag, h + 1)
                pe.wait_ge(s_kv[0], h + 1)
                for lc in range(2):
                    n = 2 * h + lc
                    if n >= 4:
                        pe.wait_ge(s_ys, n - 3)
                    out = bank[2 + n % 4][:, 0:320]
                    if lc == 0:
                        mmul(out, T[:, h, 0:P], KV[:, h % KVR, 0, :], start=True, stop=True).then_inc(s_y, 1)
                    else:
                        mmul(out, T[:, h, P:2 * P], KV[:, h % KVR, 0, :], start=True, stop=False)
                        pe.wait_ge(s_kv[1], h + 1)
                        mmul(out, T[:, h, 0:P], KV[:, h % KVR, 1, :], start=False, stop=True).then_inc(s_y, 1)

            def scores(b, g):
                n = 4 * b + g
                if n < 2:
                    pe.wait_ge(s_xtl, 4)
                else:
                    pe.wait_ge(s_max, n - 1)
                par, pairs = head_group(g)
                out = bank[n % 2]
                mmul(out[:, :], identb[:, :], maskb[:, :, :].rearrange("p h t -> p (h t)"), start=True, stop=False,
                     skip_group_check=True)
                rows = slice(64 * par, 64 * par + 64)
                for j, pair in enumerate(pairs):
                    last = mmul(out[:, P * j:P * j + P], QK[rows, 0, pair, P * b:P * b + P],
                                QK[rows, 1, pair, P * b:P * b + P], start=False, stop=(j == 3),
                                skip_group_check=True)
                last.then_inc(s_s, 1)

            def scores_t(b, g):
                n = 4 * b + g
                if n == 0:
                    pe.wait_ge(s_ys, 2 * H)
                if n >= 2:
                    pe.wait_ge(s_exp, n - 1)
                par, pairs = head_group(g)
                out = bank[2 + n % 2]
                rows = slice(64 * par, 64 * par + 64)
                mrows = slice(64 * par, 64 * par + 48)
                for j, pair in enumerate(pairs):
                    o = out[:, P * j:P * j + P]
                    mmul(o, sel[mrows, 4 * g + j, :], mT[mrows, b % 2, :], start=True, stop=False,
                         skip_group_check=True)
                    last = mmul(o, QK[rows, 1, pair, P * b:P * b + P], QK[rows, 0, pair, P * b:P * b + P],
                                start=False, stop=True, skip_group_check=True)
                last.then_inc(s_stt, 1)

            def attend(b, g):
                n = 4 * b + g
                pe.wait_ge(s_msk, n + 1)
                if g == 0:
                    if b == 0:
                        pe.wait_ge(s_ys, 2 * H)
                        pe.wait_ge(s_vs, B)
                        pe.wait_ge(s_const, 9)
                    else:
                        pe.wait_ge(s_pvs, b)
                for j in range(4):
                    last = mmul(bank[4][32 * j:32 * j + 32, P * g:P * g + P], vaug[:, b, 4 * g + j, :],
                                PT[:, n % PR, j, :], start=True, stop=True)
                last.then_inc(s_pv, 1)

            misc = [None]

            def take_misc(sem_, count):
                if misc[0]:
                    pe.wait_ge(*misc[0])
                else:
                    pe.wait_ge(s_vs, B)
                misc[0] = (sem_, count)

            xn = [B]
            for s in range(SLOTS):
                b4, b3, b2, b1, b0 = s - 4, s - 3, s - 2, s - 1, s
                if 0 <= b2 < B:
                    pe.wait_ge(s_pvs, b2 + 1)
                    if b2 == 0:
                        pe.wait_ge(s_ys, 2 * H)
                    else:
                        pe.wait_ge(s_och, 4 * (b2 - 1) + 2)
                    for g in range(4):
                        last = t_.transpose(bank[5][:, P * g:P * g + P], pvs[:, b2 % 2, P * g:P * g + P],
                                            ident[:, :])
                    last.then_inc(s_tok, 1)
                    if b2 >= 1:
                        pe.wait_ge(s_x1, b2)
                    mmul(bank[6][:, 0:272], later[:, :], vaug[:, b2, :, 0:DH + 1],
                         start=True, stop=True).then_inc(s_suf, 1)
                if b0 < B:
                    if b0 % 4 == 0:
                        for k in range(2):
                            pe.wait_ge(s_pack[b0 // 4][k], 64)
                    scores(b0, 0)
                    scores(b0, 1)
                if 0 <= b3 < B:
                    take_misc(s_qx, b3 + 1)
                    pe.wait_ge(s_xn, ln_count["ln2", b3])
                    for c in range(2):
                        last = t_.transpose(bank[7][:, P * c:P * c + P], XN[:, b3, P * c:P * c + P], ident[:, :])
                    last.then_inc(s_qt, 1)
                if 0 <= b1 < B:
                    pe.wait_ge(s_mt, b1 + 1)
                    scores_t(b1, 0)
                    scores_t(b1, 1)
                if 0 <= b4 < B:
                    take_misc(s_x2, b4 + 1)
                    pe.wait_ge(s_r, b4 + 1)
                    for c in range(2):
                        last = t_.transpose(bank[7][:, P * c:P * c + P],
                                            R[:, b4 % 2, H * c:H * c + H, :].rearrange("p h i -> p (h i)"),
                                            ident[:, :])
                    last.then_inc(s_rt, 1)
                if 0 <= b1 < B:
                    attend(b1, 0)
                if b0 < B:
                    scores(b0, 2)
                if 0 <= b1 < B:
                    scores_t(b1, 2)
                    attend(b1, 1)
                if 0 <= b2 < B:
                    take_misc(s_otl, b2 + 1)
                    pe.wait_ge(s_och, 4 * b2 + 4)
                    for c in range(2):
                        last = t_.transpose(bank[7][:, P * c:P * c + P], o_sb[:, b2 % 2, P * c:P * c + P],
                                            ident[:, :])
                    last.then_inc(s_ot, 1)
                if b0 < B:
                    scores(b0, 3)
                if 0 <= b1 < B:
                    scores_t(b1, 3)
                    attend(b1, 2)
                if 0 <= b2 < B:
                    pe.wait_ge(s_otl, b2 + 1)
                    pe.wait_ge(s_wl, 2)
                    three(bank[6][:, 0:D],
                          lambda c: oTh[:, b2 % 2, c, :], lambda c: oTl[:, b2 % 2, c, :],
                          lambda c: woh[:, c, :], lambda c: wol[:, c, :], range(2)).then_inc(s_proj, 1)
                if 0 <= b4 < B:
                    take_misc(s_ytl, b4 + 1)
                    pe.wait_ge(s_xn, ln_count["ln3", b4])
                    for c in range(2):
                        last = t_.transpose(bank[7][:, P * c:P * c + P], XN[:, b4, c::2], ident[:, :])
                    last.then_inc(s_yt, 1)
                if 0 <= b1 < B:
                    attend(b1, 3)
                if b0 < B:
                    take_misc(s_mt, b0 + 1)
                    pe.wait_ge(s_mch, 5 * b0 + 5)
                    t_.transpose(bank[7][:, 0:64].bitcast(BF16)[0:112, :], mp[:, b0 % 2, :],
                                 identb[:, :]).then_inc(s_mpt, 1)

            def gate_and_up(u):
                j, nib, g = u // 4, (u // 2) % 2, u % 2
                if u == 0:
                    pe.wait_ge(s_ffl, 1)
                    pe.wait_ge(s_max, 4 * B)
                    pe.wait_ge(s_exp, 4 * B)
                if u < 2:
                    pe.wait_ge(s_ytl, 4 * g + 4)
                if u % 4 == 0:
                    pe.wait_ge(s_ffl, j + 1)
                for w, (out, signal) in enumerate(((bank[2 * (u % 2)], s_g), (bank[2 * (u % 2) + 1], s_u))):
                    if u >= 2:
                        pe.wait_ge(s_gel if w == 0 else s_act, u - 1)
                    col = slice(256 * w + P * nib, 256 * w + P * nib + P)
                    three(out[:, :],
                          lambda c: Wh[:, j % 2, c, col], lambda c: Wl[:, j % 2, c, col],
                          lambda c: xTh[:, c, HALF * g:HALF * g + HALF],
                          lambda c: xTl[:, c, HALF * g:HALF * g + HALF], range(2)).then_inc(signal, 1)

            def down(u):
                j, nib, g = u // 4, (u // 2) % 2, u % 2
                if u == 0:
                    pe.wait_ge(s_pvs, B)
                    pe.wait_ge(s_och, 4 * B)
                    pe.wait_ge(s_x1, B)
                    pe.wait_ge(s_ytl, B)
                pe.wait_ge(s_il, u + 1)
                for tt in range(4):
                    b = 4 * g + tt
                    out = bank[4 + b // 2][:, D * (b % 2):D * (b % 2) + D]
                    t = slice(P * tt, P * tt + P)
                    for n, (a, w) in enumerate(((ih, Wh), (ih, Wl), (il, Wh))):
                        last = mmul(out, a[:, u % IR, t], w[:, j % 2, nib, 512:768],
                                    start=(u < 2 and tt % 2 == 0 and n == 0), stop=(u >= UNITS - 2 and n == 2),
                                    skip_group_check=True)
                last.then_inc(s_down, 1)

            for u in range(UNITS):
                gate_and_up(u)
                if u >= 2:
                    down(u - 2)
            down(UNITS - 2)
            down(UNITS - 1)


def kernel(x, ctx_2048, L0_attn_Wq, L0_attn_Wk, L0_attn_Wv, L0_attn_Wo, L0_xattn_ssm_kernel, L0_xattn_D,
           L0_ffn_gate_W_packed, L0_ffn_gate_scales, L0_ffn_up_W_packed, L0_ffn_up_scales,
           L0_ffn_down_W_packed, L0_ffn_down_scales):
    import numpy as np
    import concourse.bacc as bacc
    from concourse.bass_utils import run_bass_kernel_spmd

    def arr(a):
        return np.asarray(a)

    def regroup(a, axis):
        a = arr(a)
        a = np.moveaxis(a, axis, 0)
        a = a.reshape(2, 4, 2, DH, D).transpose(0, 2, 1, 3, 4).reshape(D, D)
        return np.moveaxis(a, 0, axis)

    keys = arr(ctx_2048).transpose(2, 0, 1).reshape(2, P, B, H, HD)[:, ::-1]
    keys = np.concatenate([keys, keys[..., :4]], axis=-1)

    wqkv = np.stack([arr(L0_attn_Wq), arr(L0_attn_Wk), regroup(L0_attn_Wv, 1)])
    wo = regroup(L0_attn_Wo, 0)
    kernel_rows = np.zeros((H, 384), np.float32)
    kernel_rows[:, 128:] = arr(L0_xattn_ssm_kernel)

    def by_step(rows):
        k = rows.shape[1]
        return rows.reshape(STEPS, P, 2, k).transpose(0, 3, 2, 1).reshape(STEPS, k, 2 * P)

    down_codes = arr(L0_ffn_down_W_packed).T.reshape(STEPS, P, D)
    codes = np.concatenate([by_step(arr(L0_ffn_gate_W_packed)), by_step(arr(L0_ffn_up_W_packed)), down_codes],
                           axis=2)
    gu_scale = np.concatenate([by_step(arr(L0_ffn_gate_scales)), by_step(arr(L0_ffn_up_scales))], axis=2)
    down_scale = arr(L0_ffn_down_scales).T

    nc = bacc.Bacc("TRN2", target_bir_lowering=False, num_devices=1)
    named = [("x", arr(x)), ("ctx", keys), ("wqkv", wqkv), ("wo", wo), ("ker", kernel_rows),
             ("skip", arr(L0_xattn_D)), ("gu_scale", gu_scale), ("down_scale", down_scale), ("codes", codes)]
    arrays, args = {}, []
    for name, a in named:
        a = np.ascontiguousarray(a)
        arrays[f"in_{name}"] = a
        args.append(nc.dram_tensor(f"in_{name}", a.shape, mybir.dt.from_np(a.dtype), kind="ExternalInput").ap())
    out = nc.dram_tensor("out", (B, P, D), F32, kind="ExternalOutput").ap()
    build(nc, *args, out)
    r = run_bass_kernel_spmd(nc, [arrays], core_ids=[0])
    return r.results[0]["out"]
```

```python
from contextlib import ExitStack

import concourse.bass as bass
from concourse import mybir

F32, F16, BF16, I32 = mybir.dt.float32, mybir.dt.float16, mybir.dt.bfloat16, mybir.dt.int32
ACT = mybir.ActivationFunctionType
ALU = mybir.AluOpType
AX = mybir.AxisListType

P = 128
B = 8
D = 256
NC_ = D // P
H = 16
DH = D // H
HD = 8
NPAIR = 5
NSLOT = 9
MLP = 2048
STEPS = MLP // D
UNITS = STEPS * 4
RW = 4
HALF = 512
EPS = 1e-5
SCALE = 1.0 / 128 ** 0.5
NEG = -1.0e30
W_GAIN = 16.0
DECODE_GAIN = 2.0 ** 14 * W_GAIN
GELU_A, GELU_B = 0.7978845608028654, 0.044715
GATE_K = W_GAIN ** 2 / GELU_B
TANH_SCALE = GELU_A * GELU_B / W_GAIN ** 3
UP_SCALE = 0.5 / W_GAIN ** 2


def build(nc, x_d, ctx_d, wqkv_d, wo_d, ker_d, skip_d, gu_scale_d, down_scale_d, codes_d, out_d):
    scr = nc.dram_tensor("qk_scratch", (2, 2, H, 3, DH, HALF), F16, kind="Internal").ap()

    ctx = ExitStack()
    with ctx:
        def sb(name, shape, dt=F32):
            return ctx.enter_context(nc.sbuf_tensor(name, shape, dt))

        def sem(name):
            return ctx.enter_context(nc.semaphore(name))

        def view(ap, dims, offset=0):
            return bass.AP(ap.tensor, ap.offset + offset, [list(ap.ap[0])] + [list(d) for d in dims])

        X = sb("X", [P, B, D])
        XN = sb("XN", [P, B, D])
        xTh = sb("xTh", [P, NC_, B * P], F16)
        xTl = sb("xTl", [P, NC_, B * P], F16)
        wqkvh = sb("wqkvh", [P, NC_, 3, D], F16)
        wqkvl = sb("wqkvl", [P, NC_, 3, D], F16)
        wo = sb("wo", [P, NC_, D])
        Ys = sb("Ys", [P, H, 2, B, NPAIR * HD])
        early = Ys[:, :, :, :, :].rearrange("p a b c d -> p (a b c d)")
        wqkv32 = early[:, 4608:6144].rearrange("p (c w n) -> p c w n", c=NC_, w=3)
        nat = early[:, 6144:10240].bitcast(F16).rearrange(
            "p (g k m s t) -> p g k m s t", g=2, k=2, m=2, s=2)
        STAGING_HEAD = 4096 // (2 * B * NPAIR * HD)
        arena = sb("arena", [P, 9728])
        kx = arena[:, 0:3072].rearrange("p (m b h i) -> p m b h i", m=2, b=B, h=H)
        KVR = 4
        KV = arena[:, 3072:5632].rearrange("p (r m n) -> p r m n", r=KVR, m=2)
        T = arena[:, 5632:9728].rearrange("p (h l) -> p h l", h=H)
        Z = arena[:, 0:4608].rearrange("p (r h s) -> p r h s", r=2, h=2 * H)
        codes = arena[:, 5632:7168].bitcast(I32).rearrange("p (r n) -> p r n", r=2)
        scales = arena[:, 7168:8704].rearrange("p (r n) -> p r n", r=2)
        bits = arena[:, 8704:9472].bitcast(I32)
        Wa = sb("Wa", [P, 4, 2, 768], F16)
        QK = sb("QK", [P, 2, H // 2, B * P], F16)
        late = QK[:, :, :, :].rearrange("p a b c -> p (a b c)").bitcast(F32)
        sq = late[:, 0:1024].rearrange("p (r t) -> p r t", r=2)
        poly = late[:, 1024:2048].rearrange("p (r t) -> p r t", r=2)
        th = late[:, 2048:3072].rearrange("p (r t) -> p r t", r=2)
        gel = late[:, 3072:4096].rearrange("p (r t) -> p r t", r=2)
        act = late[:, 4096:5120].rearrange("p (r t) -> p r t", r=2)
        IR = 4
        ih = late[:, 5120:6144].bitcast(F16).rearrange("p (r t) -> p r t", r=IR)
        il = late[:, 6144:7168].bitcast(F16).rearrange("p (r t) -> p r t", r=IR)
        bits2 = late[:, 7168:7936].bitcast(I32)
        vaug = sb("vaug", [P, B, H, 32])
        Wb = vaug[:, :, :, :].rearrange("p b h d -> p (b h d)").bitcast(F16)[:, 0:6144].rearrange(
            "p (s n w) -> p s n w", s=4, n=2)
        Wh = [Wa[:, 0], Wa[:, 1], Wb[:, 0], Wb[:, 1]]
        Wl = [Wa[:, 2], Wa[:, 3], Wb[:, 2], Wb[:, 3]]
        PR = 4
        PT = sb("PT", [P, PR, 4, P])
        W32 = PT[:, 0:3, :, :].rearrange("p a b c -> p (a b c)").rearrange("p (n w) -> p n w", n=2)
        pvs = sb("pvs", [P, 2, 512])
        tail = sb("tail", [P, H, DH + 1])
        num = sb("num", [P, H, DH + 1])
        rec = sb("rec", [P, H])
        o_sb = sb("o_sb", [P, 2, D])
        oT = sb("oT", [P, 2, NC_, P])
        qx = sb("qx", [P, 2, 2 * H, 12])
        R = sb("R", [P, 2, 2 * H, HD])
        stats = sb("stats", [P, B, 6])
        mv = sb("mv", [P, B, 2])
        veps = sb("veps", [P, B])
        shift = sb("shift", [P, B])
        rstd = sb("rstd", [P, B])
        nhalf = sb("nhalf", [P, B])
        mx = sb("mx", [P, 2, H])
        mm = sb("mm", [P, 2, H])
        res1 = sb("res1", [P, H])
        res2 = sb("res2", [P, H])
        mp = sb("mp", [P, 2, 112], BF16)
        mT = sb("mT", [112, 2, P], BF16)
        em = sb("em", [P, 4, H])
        ident = sb("ident", [P, P])
        anti = sb("anti", [P, P])
        identb = sb("identb", [P, P], BF16)
        later = sb("later", [P, P])
        maskb = sb("maskb", [P, 4, P], BF16)
        sel = sb("sel", [112, H, P], BF16)
        sel_row = sb("sel_row", [112, H], BF16)
        guard = sb("guard", [P, 1])
        skip = sb("skip", [P, H])

        bank = [ctx.enter_context(nc.psum_tensor(f"bank{i}", [P, 512], F32)) for i in range(8)]

        s_x = [sem(f"s_xin{pr}") for pr in range(4)]
        s_w = [sem(f"s_w{c}") for c in "qkvo"]
        s_skip = sem("s_skip")
        s_sel = sem("s_sel")
        s_ctx = [sem(f"s_ctx{g}") for g in range(2)]
        s_toep = [sem(f"s_toep{g}") for g in range(2)]
        s_const = sem("s_const")
        s_zero = sem("s_zero")
        s_st = [sem(f"s_st{n}") for n in range(3)]
        s_mv = [sem(f"s_mv{n}") for n in range(3)]
        s_rstd = [sem(f"s_rstd{n}") for n in range(3)]
        s_xn = [sem(f"s_xn{n}") for n in range(3)]
        s_xt = sem("s_xt")
        s_xth, s_xtl = sem("s_xth"), sem("s_xtl")
        s_wh, s_wl = sem("s_wh"), sem("s_wl")
        s_qk = sem("s_qk")
        s_qkh, s_qkl = sem("s_qkh"), sem("s_qkl")
        s_scr = [sem(f"s_scr{i}") for i in range(4)]
        s_pack = [[sem(f"s_pack{g}{k}") for k in range(2)] for g in range(2)]
        s_v, s_vs = sem("s_v"), sem("s_vs")
        s_tdiag = sem("s_tdiag")
        s_kv = [sem("s_kv0"), sem("s_kv1")]
        s_y, s_ys = [sem(f"s_y{c}") for c in range(2)], [sem(f"s_ys{c}") for c in range(2)]
        s_s, s_max = sem("s_s"), sem("s_max")
        s_mch = sem("s_mch")
        s_em = sem("s_em")
        s_mpt = sem("s_mpt")
        s_mt = sem("s_mt")
        s_stt = sem("s_stt")
        s_exp, s_msk, s_pv = sem("s_exp"), sem("s_msk"), sem("s_pv")
        s_pvs, s_tok, s_suf = sem("s_pvs"), sem("s_tok"), sem("s_suf")
        s_och = sem("s_och")
        s_ot, s_ott, s_proj, s_x1 = sem("s_ot"), sem("s_ott"), sem("s_proj"), sem("s_x1")
        s_qt, s_qx, s_z, s_r = sem("s_qt"), sem("s_qx"), sem("s_z"), sem("s_r")
        s_rt, s_x2 = sem("s_rt"), sem("s_x2")
        s_yt, s_yth, s_ytl = sem("s_yt"), sem("s_yth"), sem("s_ytl")
        s_code = [sem(f"s_code{r}") for r in range(2)]
        s_bits = sem("s_bits")
        s_w32, s_ffh, s_ffl = sem("s_w32"), sem("s_ffh"), sem("s_ffl")
        s_g, s_u, s_sq, s_poly, s_th = sem("s_g"), sem("s_u"), sem("s_sq"), sem("s_poly"), sem("s_th")
        s_gel, s_act, s_ih, s_il, s_down = sem("s_gel"), sem("s_act"), sem("s_ih"), sem("s_il"), sem("s_down")
        s_fin, s_out = sem("s_fin"), sem("s_out")
        block = ctx.enter_context(nc.Block())

        (T_SCORES, T_SPLIT, T_MPT, T_ST, T_MASK, T_ATT, T_PVOUT, T_TOK, T_NORM, T_OT, T_PROJ, T_LN2, T_RSTD2,
         T_APPLY2, T_QT, T_MIX, T_SUM, T_SUM2, T_RT, T_LN3, T_RSTD3, T_APPLY3, T_YT) = (
            0, 4, 5, 7, 8, 9, 13, 14, 15, 16, 18, 19, 20, 21, 23, 24, 27, 27, 29, 30, 31, 32, 35)
        TICKS = 4 * (B - 1) + T_YT + 2
        CONV_EARLY = 4
        CONV_RATE = 1
        T_UNIT, UNIT_EVERY, EARLY = 48, 2, 4
        T_ZERO = 22
        T_DECODE = 40
        DECODE_AHEAD = 6

        ORDER = ([(j, n, g) for g in range(2) for j in range(EARLY) for n in range(2)]
                 + [(j, n, g) for j in range(EARLY, STEPS) for n in range(2) for g in range(2)])
        last_of = {j: u for u, (j, _, _) in enumerate(ORDER)}

        def early_units(t):
            n, rest = divmod(t - T_UNIT, UNIT_EVERY)
            return [n] if rest == 0 and 0 <= n < 2 * EARLY else []

        def early_decode(t, at):
            j, rest = divmod(t - T_DECODE - at, 4)
            return [j] if rest == 0 and 0 <= j < EARLY else []

        def late_decode(u, at):
            j, rest = divmod(u - at + DECODE_AHEAD, 4)
            return [j] if rest == 0 and EARLY <= j < STEPS else []

        def batch(t, at):
            b, r = divmod(t - at, 4)
            return [b] if r == 0 and 0 <= b < B else []

        def group(t, at):
            n = t - at
            return [divmod(n, 4)] if 0 <= n < 4 * B else []

        def conv_heads(t):
            return [h for h in range(CONV_EARLY + CONV_RATE * t, CONV_EARLY + CONV_RATE * (t + 1)) if h < H]

        def conv_bank(h, lc):
            return bank[2 + (2 * h + lc) % 4] if h < CONV_EARLY else bank[6 + lc]

        def head_group(g):
            return g % 2, [4 * (g // 2) + j for j in range(4)]

        @block.sync
        def _(sp):
            def load_x(pr, n):
                sp.dma_start(X[:, 2 * pr:2 * pr + 2 * n, :],
                             x_d[2 * pr:2 * pr + 2 * n].rearrange("b t d -> t b d")).then_inc(s_x[pr], 16)

            def load_w(w):
                sp.dma_start(wqkv32[:, :, w, :],
                             wqkv_d[w].rearrange("(c p) n -> p c n", p=P)).then_inc(s_w[w], 16)

            load_x(0, 1)
            load_w(0)
            load_x(1, 1)
            load_w(1)
            load_x(2, 2)
            load_w(2)
            for m in range(2):
                sp.dma_start(kx[:, m], ctx_d[m]).then_inc(s_ctx[m], 16)
            sp.dma_start(skip[:, :], bass.AP(skip_d.tensor, skip_d.offset, [[0, P], [1, H]])).then_inc(s_skip, 16)
            for g in range(2):
                sp.dma_start(T[:, 8 * g:8 * g + 8, :],
                             bass.AP(ker_d.tensor, ker_d.offset + 1 + 8 * g * 384,
                                     [[1, P], [384, 8], [1, D]])).then_inc(s_toep[g], 16)
            sp.dma_start(wo[:, :, :], wo_d.rearrange("(c p) n -> p c n", p=P)).then_inc(s_w[3], 16)
            for g in range(2):
                for k in range(2):
                    sp.wait_ge(s_qkl, 4 * g + 2 * k + 2)
                    for m in range(2):
                        for part in range(3 if k == 0 else 2):
                            sp.dma_start(scr[g, k, 8 * m:8 * m + 8, part],
                                         nat[:, g, k, m, part % 2, :]).then_inc(s_scr[2 * g + k], 16)
                for k in range(2):
                    sp.wait_ge(s_scr[2 * g + k], 96 if k == 0 else 64)
                    for par in range(2):
                        for two in range(2):
                            first = 1 if k == 0 and two else 0
                            src = scr[g, k, par::2, first:first + 2].rearrange("h s d t -> (s d) h t")
                            rows = 64 * par + 32 * two
                            sp.dma_start(QK[rows:rows + 32, k, :, HALF * g:HALF * g + HALF],
                                         src).then_inc(s_pack[g][k], 16)

            def load_codes(j):
                r = j % 2
                if j == 0:
                    for lc in range(2):
                        sp.wait_ge(s_y[lc], H)
                if j >= 2:
                    sp.wait_ge(s_w32, j - 1)
                sp.dma_start(codes[:, r, :], codes_d[j]).then_inc(s_code[r], 16)
                sp.dma_start(scales[:, r, 0:512], bass.AP(
                    gu_scale_d.tensor, gu_scale_d.offset + j * 8 * 512,
                    [[512, 8], [0, 16], [1, 512]])).then_inc(s_code[r], 16)
                sp.dma_start(scales[:, r, 512:768], bass.AP(
                    down_scale_d.tensor, down_scale_d.offset + j * 8 * D,
                    [[D, 8], [0, 16], [1, D]])).then_inc(s_code[r], 16)

            for j in range(STEPS):
                load_codes(j)
            for b in range(B):
                sp.wait_ge(s_fin, b + 1)
                sp.dma_start(out_d[b], XN[:, b, :]).then_inc(s_out, 16)
            sp.wait_ge(s_out, 16 * B)

        @block.gpsimd
        def _(pool):
            g_ = nc.gpsimd
            z = [0]

            def own(ins):
                z[0] += 1
                ins.then_inc(s_zero, 1)
                pool.wait_ge(s_zero, z[0])

            own(g_.memset(ident[:, :], 0.0))
            g_.affine_select(out=ident[:, :], in_=ident[:, :], compare_op=ALU.not_equal, fill=1.0, base=0,
                             pattern=[[-1, P]], channel_multiplier=1).then_inc(s_const, 1)
            own(g_.memset(anti[:, :], 0.0))
            g_.affine_select(out=anti[:, :], in_=anti[:, :], compare_op=ALU.not_equal, fill=1.0,
                             base=-(P - 1), pattern=[[1, P]], channel_multiplier=1).then_inc(s_const, 1)
            own(g_.memset(nhalf[:, :], -0.5))

            def rstds(ln, n0, n):
                own(g_.tensor_scalar(veps[:, n0:n0 + n], mv[:, n0:n0 + n, 1], EPS, None, ALU.add))
                if ln == 0:
                    g_.tensor_tensor(rstd[:, n0:n0 + n], veps[:, n0:n0 + n], nhalf[:, n0:n0 + n],
                                     ALU.pow).then_inc(s_rstd[ln], n)
                else:
                    own(g_.tensor_tensor(rstd[:, n0:n0 + n], veps[:, n0:n0 + n], nhalf[:, n0:n0 + n], ALU.pow))
                    g_.tensor_scalar(shift[:, n0:n0 + 1], mv[:, n0:n0 + 1, 0], rstd[:, n0:n0 + 1], -1.0,
                                     ALU.mult, ALU.mult).then_inc(s_rstd[ln], 1)

            for n0, n in ((0, 2), (2, 2), (4, 4)):
                pool.wait_ge(s_mv[0], n0 + n)
                rstds(0, n0, n)
                if n0 == 2:
                    g_.memset(vaug[:, :, :, DH:DH + 1], 1.0).then_inc(s_const, 1)
                    g_.memset(vaug[:, :, :, DH + 1:32], 0.0).then_inc(s_const, 1)
            own(g_.memset(maskb[:, :, :], 0.0))
            g_.affine_select(out=maskb[:, :, :], in_=maskb[:, :, :], compare_op=ALU.is_ge, fill=NEG, base=0,
                             pattern=[[0, 4], [-1, P]], channel_multiplier=1).then_inc(s_const, 1)
            own(g_.memset(identb[:, :], 0.0))
            g_.affine_select(out=identb[:, :], in_=identb[:, :], compare_op=ALU.not_equal, fill=1.0, base=0,
                             pattern=[[-1, P]], channel_multiplier=1).then_inc(s_const, 1)

            def products(h):
                m = 1
                if h >= KVR:
                    for lc in range(2):
                        pool.wait_ge(s_y[lc], h - KVR + 1)
                a = kx[:, m, :, h, :]
                g_.tensor_tensor(
                    view(KV[:, h % KVR, m, :], [[40, B], [8, NPAIR], [1, HD]]),
                    view(a, [[12 * H, B], [0, NPAIR], [1, HD]]),
                    view(a, [[12 * H, B], [1, NPAIR], [1, HD]]), ALU.mult).then_inc(s_kv[1], 1)

            pool.wait_ge(s_ctx[1], 16)
            for h in range(max(KVR, CONV_EARLY)):
                products(h)

            own(g_.memset(later[:, :], 1.0))
            g_.affine_select(out=later[:, :], in_=later[:, :], compare_op=ALU.is_gt, fill=0.0, base=0,
                             pattern=[[-1, P]], channel_multiplier=1).then_inc(s_const, 1)
            own(g_.memset(guard[:, :], 0.0))
            own(g_.affine_select(out=guard[:, :], in_=guard[:, :], compare_op=ALU.not_equal, fill=NEG,
                                 base=-(P - 1), pattern=[[0, 1]], channel_multiplier=1))
            own(g_.memset(sel_row[:, :], 0.0))
            for first in (0, 16, 32, 64, 80, 96):
                own(g_.affine_select(out=sel_row[:, :], in_=sel_row[:, :], compare_op=ALU.not_equal, fill=-1.0,
                                     base=-first, pattern=[[-1, H]], channel_multiplier=1))
            g_.memset(mp[:, 0, 48:64], 0.0).then_inc(s_const, 1)
            g_.memset(mp[:, 1, 48:64], 0.0).then_inc(s_const, 1)

            def mask(b, g):
                n = 4 * b + g
                pool.wait_ge(s_exp, n + 1)
                g_.affine_select(out=PT[:, n % PR], in_=PT[:, n % PR], compare_op=ALU.is_ge, fill=0.0, base=0,
                                 pattern=[[0, 4], [1, P]], channel_multiplier=-1).then_inc(s_msk, 1)

            def conv_products(b):
                r = b % 2
                pool.wait_ge(s_qx, 2 * b + 2)
                for lc in range(2):
                    pool.wait_ge(s_ys[lc], H)
                if b >= 2:
                    pool.wait_ge(s_r, 2 * (b - 1))
                g_.tensor_tensor(view(Z[:, r], [[8 * NSLOT, 2 * H], [8, NPAIR], [1, HD]]),
                                 view(early, [[40 * B, 2 * H], [8, NPAIR], [1, HD]], 40 * b),
                                 view(qx[:, r], [[12, 2 * H], [1, NPAIR], [1, HD]]), ALU.mult).then_inc(s_z, 1)
                g_.tensor_tensor(view(Z[:, r], [[8 * NSLOT, 2 * H], [HD + 1, 3], [1, HD]], 8 * NPAIR + 1),
                                 view(early, [[40 * B, 2 * H], [8, 3], [1, HD]], 40 * b + 8),
                                 view(qx[:, r], [[12, 2 * H], [0, 3], [1, HD]]), ALU.mult).then_inc(s_z, 1)

            def decode_scale(j):
                pool.wait_ge(s_bits, 4 * j + 4)
                pool.wait_ge(s_code[j % 2], 48 * (j // 2 + 1))
                if j == 0:
                    pool.wait_ge(s_pv, 4 * B)
                else:
                    pool.wait_ge(s_ffl, j)
                g_.tensor_tensor(W32[:, :, :],
                                 view(bits[:, :].bitcast(F16), [[1, 2], [2, 768]]),
                                 view(scales[:, j % 2, :], [[0, 2], [1, 768]]), ALU.mult).then_inc(s_w32, 1)

            def act_lo(u):
                pool.wait_ge(s_ih, u + 1)
                if u >= IR:
                    pool.wait_ge(s_down, u - IR + 1)
                g_.tensor_tensor(il[:, u % IR], act[:, u % 2], ih[:, u % IR], ALU.subtract).then_inc(s_il, 1)

            for t in range(TICKS):
                for j in early_decode(t, 1):
                    decode_scale(j)
                for h in conv_heads(t):
                    if h >= KVR:
                        products(h)
                if t == T_ZERO:
                    for lc in range(2):
                        pool.wait_ge(s_y[lc], H)
                    own(g_.memset(Z, 0.0))
                for b, g in group(t, T_MASK):
                    mask(b, g)
                for b in batch(t, T_RSTD3):
                    pool.wait_ge(s_mv[2], b + 1)
                    rstds(2, b, 1)
                for b in batch(t, T_RSTD2):
                    pool.wait_ge(s_mv[1], b + 1)
                    rstds(1, b, 1)
                for b in batch(t, T_MIX):
                    conv_products(b)
                for u in early_units(t):
                    if u >= 1:
                        act_lo(u - 1)
            for u in range(2 * EARLY - 1, UNITS):
                for j in late_decode(u, 1):
                    decode_scale(j)
                act_lo(u)

        @block.scalar
        def _(sc):
            s_ = nc.scalar
            def weight_hi(w):
                sc.wait_ge(s_w[w], 16)
                s_.activation(wqkvh[:, :, w, :], wqkv32[:, :, w, :], ACT.Copy).then_inc(s_wh, 1)

            def x_hi(g):
                for pr in range(2 * g, 2 * g + 2):
                    sc.wait_ge(s_xt, pr + 1)
                    s_.activation(xTh[:, :, 256 * pr:256 * pr + 256].rearrange("p c (b t) -> p b c t", b=2),
                                  bank[pr % 2][:, :].rearrange("p (b c t) -> p b c t", b=2, c=2),
                                  ACT.Copy).then_inc(s_xth, 1)

            def q_hi(g):
                for n in range(4):
                    sc.wait_ge(s_qk, 4 * g + n + 1)
                    s_.activation(nat[:, g, n // 2, n % 2, 0, :], bank[2 + n][:, :],
                                  ACT.Copy).then_inc(s_qkh, 1)

            def v_out(g):
                for b in range(4 * g, 4 * g + 4):
                    sc.wait_ge(s_v, b + 1)
                    s_.activation(vaug[:, b, :, 0:DH],
                                  bank[6 + b % 2][:, 0:D].rearrange("p (h d) -> p h d", h=H),
                                  ACT.Copy).then_inc(s_vs, 1)

            weight_hi(0)
            weight_hi(1)
            x_hi(0)
            weight_hi(2)
            q_hi(0)
            x_hi(1)
            v_out(0)
            q_hi(1)
            v_out(1)
            sc.wait_ge(s_const, 9)
            s_.activation(sel[:, :, :], view(sel_row[:, :], [[1, H], [0, P]]), ACT.Copy).then_inc(s_sel, 1)
            def conv_out(h, lc):
                if h == STAGING_HEAD and lc == 0:
                    sc.wait_ge(s_wl, 3)
                    for g in range(2):
                        for k in range(2):
                            sc.wait_ge(s_scr[2 * g + k], 96 if k == 0 else 64)
                sc.wait_ge(s_y[lc], h + 1)
                s_.activation(Ys[:, h, lc],
                              conv_bank(h, lc)[:, 0:320].rearrange("p (b k) -> p b k", b=B),
                              ACT.Copy).then_inc(s_ys[lc], 1)


            def exp_max(b):
                sc.wait_ge(s_mch, 5 * b + 1)
                if b >= 4:
                    sc.wait_ge(s_och, 4 * (b - 4) + 1)
                s_.activation(em[:, b % 4, :], mm[:, b % 2, :], ACT.Exp, scale=-SCALE).then_inc(s_em, 1)

            def probs(b, g):
                n = 4 * b + g
                sc.wait_ge(s_stt, n + 1)
                if n >= PR:
                    sc.wait_ge(s_pv, n - PR + 1)
                s_.activation(PT[:, n % PR].rearrange("p a b -> p (a b)"), bank[2 + n % 2][:, :],
                              ACT.Exp, scale=SCALE).then_inc(s_exp, 1)

            def pv_out(b):
                sc.wait_ge(s_pv, 4 * b + 4)
                if b >= 2:
                    sc.wait_ge(s_tok, b - 1)
                s_.activation(pvs[:, b % 2, :], bank[4 + b % 2][:, :], ACT.Copy).then_inc(s_pvs, 1)

            def w_hi_step(j):
                sc.wait_ge(s_w32, j + 1)
                if j == 2:
                    sc.wait_ge(s_suf, B)
                    sc.wait_ge(s_pv, 4 * B)
                if j >= RW:
                    sc.wait_ge(s_down, last_of[j - RW] + 1)
                s_.activation(Wh[j % RW], W32[:, :, :], ACT.Copy, scale=DECODE_GAIN).then_inc(s_ffh, 1)

            def act_hi(u):
                sc.wait_ge(s_act, u + 1)
                if u >= IR:
                    sc.wait_ge(s_down, u - IR + 1)
                s_.activation(ih[:, u % IR], act[:, u % 2], ACT.Copy).then_inc(s_ih, 1)

            def unit(u):
                sc.wait_ge(s_g, u + 1)
                if u >= 2:
                    sc.wait_ge(s_poly, u - 1)
                s_.activation(sq[:, u % 2], bank[2 * (u % 2)][:, :], ACT.Square).then_inc(s_sq, 1)
                if u >= 1:
                    act_hi(u - 1)
                sc.wait_ge(s_poly, u + 1)
                if u >= 2:
                    sc.wait_ge(s_gel, u - 1)
                s_.activation(th[:, u % 2], poly[:, u % 2], ACT.Tanh, scale=TANH_SCALE).then_inc(s_th, 1)

            def ln_apply(ln, b):
                sc.wait_ge(s_rstd[ln], b + 1)
                s_.activation(XN[:, b, :], X[:, b, :], ACT.Identity, bias=shift[:, b:b + 1],
                              scale=rstd[:, b:b + 1]).then_inc(s_xn[ln], 1)

            for h in range(CONV_EARLY):
                for lc in range(2):
                    conv_out(h, lc)
            for t in range(TICKS):
                for b in batch(t, T_APPLY2):
                    ln_apply(1, b)
                for b in batch(t, T_APPLY3):
                    ln_apply(2, b)
                for b in batch(t, T_PVOUT):
                    pv_out(b)
                for b in batch(t, T_OT):
                    sc.wait_ge(s_ot, b + 1)
                    if b >= 2:
                        sc.wait_ge(s_proj, b - 1)
                    s_.activation(oT[:, b % 2], bank[7][:, 0:D].rearrange("p (c t) -> p c t", c=2),
                                  ACT.Copy).then_inc(s_ott, 1)
                for b in batch(t, T_YT):
                    sc.wait_ge(s_yt, b + 1)
                    s_.activation(xTh[:, :, P * b:P * b + P],
                                  bank[6][:, 0:D].rearrange("p (c t) -> p c t", c=2),
                                  ACT.Copy).then_inc(s_yth, 1)
                for b in batch(t, T_MPT):
                    exp_max(b)
                    sc.wait_ge(s_mpt, b + 1)
                    if b >= 2:
                        sc.wait_ge(s_stt, 4 * (b - 2) + 4)
                    s_.activation(mT[:, b % 2, :], bank[7][:, 0:64].bitcast(BF16)[0:112, :],
                                  ACT.Copy).then_inc(s_mt, 1)
                for b, g in group(t, T_ST):
                    probs(b, g)
                for b in batch(t, T_QT):
                    sc.wait_ge(s_qt, b + 1)
                    if b >= 2:
                        sc.wait_ge(s_z, 2 * (b - 2) + 2)
                    s_.activation(view(qx[:, b % 2], [[12, 2], [24, H], [1, 4]], 8),
                                  view(bank[7][:, :], [[P, 2], [8, H], [1, 4]]),
                                  ACT.Copy).then_inc(s_qx, 1)
                    s_.activation(view(qx[:, b % 2], [[12, 2], [24, H], [1, HD]]),
                                  view(bank[7][:, :], [[P, 2], [8, H], [1, HD]]),
                                  ACT.Copy).then_inc(s_qx, 1)
                for h in conv_heads(t):
                    conv_out(h, 0)
                for h in conv_heads(t):
                    conv_out(h, 1)
                for u in early_units(t):
                    unit(u)
                for j in early_decode(t, 2):
                    w_hi_step(j)
            for u in range(2 * EARLY, UNITS):
                unit(u)
                for j in late_decode(u, 2):
                    w_hi_step(j)
            act_hi(UNITS - 1)

        @block.vector
        def _(ve):
            v_ = nc.vector
            def ln_stats(ln, b):
                v_.bn_stats(out=stats[:, b, :], in_=X[:, b, :]).then_inc(s_st[ln], 1)
                ve.wait_ge(s_st[ln], b + 1)
                v_.bn_aggr(out=mv[:, b, :], in_=stats[:, b, :]).then_inc(s_mv[ln], 1)

            def ln_apply(ln, b, n):
                ve.wait_ge(s_rstd[ln], n)
                v_.tensor_scalar(XN[:, b, :], X[:, b, :], mv[:, b, 0:1], rstd[:, b:b + 1],
                                 ALU.subtract, ALU.mult).then_inc(s_xn[ln], 1)

            def x_lo(pr):
                ve.wait_ge(s_xth, pr + 1)
                v_.tensor_tensor(xTl[:, :, 256 * pr:256 * pr + 256].rearrange("p c (b t) -> p b c t", b=2),
                                 bank[pr % 2][:, :].rearrange("p (b c t) -> p b c t", b=2, c=2),
                                 xTh[:, :, 256 * pr:256 * pr + 256].rearrange("p c (b t) -> p b c t", b=2),
                                 ALU.subtract).then_inc(s_xtl, 1)

            def weight_lo(w):
                ve.wait_ge(s_wh, w + 1)
                v_.tensor_tensor(wqkvl[:, :, w, :], wqkv32[:, :, w, :], wqkvh[:, :, w, :],
                                 ALU.subtract).then_inc(s_wl, 1)

            for b in range(4):
                if b % 2 == 0:
                    ve.wait_ge(s_x[b // 2], 16)
                ln_stats(0, b)
            for pr in range(2):
                for b in (2 * pr, 2 * pr + 1):
                    ln_apply(0, b, 2 * pr + 2)
                weight_lo(pr)
            x_lo(0)
            x_lo(1)
            ve.wait_ge(s_x[2], 16)
            for b in range(4, B):
                ln_stats(0, b)
            weight_lo(2)
            for b in range(4, B):
                ln_apply(0, b, B)

            def q_lo(g):
                for n in range(4):
                    ve.wait_ge(s_qkh, 4 * g + n + 1)
                    v_.tensor_tensor(nat[:, g, n // 2, n % 2, 1, :], bank[2 + n][:, :],
                                     nat[:, g, n // 2, n % 2, 0, :], ALU.subtract).then_inc(s_qkl, 1)

            def products(h):
                if h == 0:
                    ve.wait_ge(s_ctx[0], 16)
                if h >= KVR:
                    for lc in range(2):
                        ve.wait_ge(s_y[lc], h - KVR + 1)
                a = kx[:, 0, :, h, :]
                v_.tensor_tensor(view(KV[:, h % KVR, 0, :], [[40, B], [8, NPAIR], [1, HD]]),
                                 view(a, [[12 * H, B], [0, NPAIR], [1, HD]]),
                                 view(a, [[12 * H, B], [1, NPAIR], [1, HD]]), ALU.mult).then_inc(s_kv[0], 1)

            def skip_tap(h):
                if h == 0:
                    ve.wait_ge(s_skip, 16)
                    ve.wait_ge(s_const, 2)
                if h % 8 == 0:
                    ve.wait_ge(s_toep[h // 8], 16)
                v_.scalar_tensor_tensor(out=T[:, h, 0:P], in0=anti[:, :], scalar=skip[:, h:h + 1],
                                        in1=T[:, h, 0:P], op0=ALU.mult, op1=ALU.add).then_inc(s_tdiag, 1)

            q_lo(0)
            x_lo(2)
            x_lo(3)
            for h in range(KVR):
                products(h)
            for h in range(8):
                skip_tap(h)
            q_lo(1)
            for h in range(8, H):
                skip_tap(h)
            for h in range(KVR, CONV_EARLY):
                products(h)

            def group_max(b, g):
                n = 4 * b + g
                ve.wait_ge(s_s, n + 1)
                v_.tensor_reduce(mx[:, b % 2, 4 * g:4 * g + 4],
                                 bank[n % 2][:, :].rearrange("p (h t) -> p h t", h=4),
                                 AX.X, ALU.max).then_inc(s_max, 1)

            def split_max(b):
                r = b % 2
                ve.wait_ge(s_max, 4 * b + 4)
                if b == 0:
                    ve.wait_ge(s_const, 9)
                if b >= 2:
                    ve.wait_ge(s_em, b - 1)
                v_.tensor_scalar(mm[:, r, :], mx[:, r, :], guard[:, 0:1], None, ALU.max).then_inc(s_mch, 1)
                ve.wait_ge(s_mch, 5 * b + 1)
                if b >= 2:
                    ve.wait_ge(s_mpt, b - 1)

                def twice(part):
                    return view(mp[:, r, :], [[64, 2], [1, H]], 16 * part)

                def rep(t):
                    return view(t, [[0, 2], [1, H]])

                v_.tensor_copy(twice(0), rep(mm[:, r, :])).then_inc(s_mch, 1)
                ve.wait_ge(s_mch, 5 * b + 2)
                v_.tensor_tensor(res1[:, :], mm[:, r, :], mp[:, r, 0:16], ALU.subtract).then_inc(s_mch, 1)
                ve.wait_ge(s_mch, 5 * b + 3)
                v_.tensor_copy(twice(1), rep(res1[:, :])).then_inc(s_mch, 1)
                ve.wait_ge(s_mch, 5 * b + 4)
                v_.tensor_tensor(twice(2), rep(res1[:, :]), rep(mp[:, r, 16:32]),
                                 ALU.subtract).then_inc(s_mch, 1)

            def normalise(b):
                ve.wait_ge(s_suf, b + 1)
                ve.wait_ge(s_em, b + 1)
                v_.tensor_tensor(tail[:, :, :], bank[6][:, 0:272].rearrange("p (h d) -> p h d", h=H),
                                 view(em[:, b % 4, :], [[1, H], [0, DH + 1]]), ALU.mult).then_inc(s_och, 1)
                ve.wait_ge(s_och, 4 * b + 1)
                ve.wait_ge(s_tok, b + 1)
                v_.tensor_tensor(num[:, :, :], tail[:, :, :], view(bank[4 + b % 2][:, :], [[32, H], [1, DH + 1]]),
                                 ALU.add).then_inc(s_och, 1)
                ve.wait_ge(s_och, 4 * b + 2)
                v_.reciprocal(rec[:, :], num[:, :, DH]).then_inc(s_och, 1)
                ve.wait_ge(s_och, 4 * b + 3)
                v_.tensor_tensor(o_sb[:, b % 2, :].rearrange("p (h d) -> p h d", h=H), num[:, :, 0:DH],
                                 view(rec[:, :], [[1, H], [0, DH]]), ALU.mult).then_inc(s_och, 1)

            def codes_bits(j):
                r = j % 2
                ve.wait_ge(s_code[r], 48 * (j // 2 + 1))
                if j == 0:
                    ve.wait_ge(s_stt, 4 * B)
                v_.scalar_tensor_tensor(out=bits2[:, :], in0=codes[:, r, :], scalar=12, in1=codes[:, r, :],
                                        op0=ALU.logical_shift_left, op1=ALU.bitwise_or).then_inc(s_bits, 1)
                ve.wait_ge(s_bits, 4 * j + 1)
                if j >= 1:
                    ve.wait_ge(s_w32, j)
                v_.tensor_scalar(codes[:, r, :], bits2[:, :], 0x00070007, 9, ALU.bitwise_and,
                                 ALU.logical_shift_left).then_inc(s_bits, 1)
                v_.tensor_scalar(bits[:, :], bits2[:, :], 0x00080008, 12, ALU.bitwise_and,
                                 ALU.logical_shift_left).then_inc(s_bits, 1)
                ve.wait_ge(s_bits, 4 * j + 3)
                v_.tensor_tensor(bits[:, :], bits[:, :], codes[:, r, :], ALU.bitwise_or).then_inc(s_bits, 1)

            def w_lo(j):
                ve.wait_ge(s_ffh, j + 1)
                v_.scalar_tensor_tensor(out=Wl[j % RW].rearrange("p a b -> p (a b)"),
                                        in0=W32[:, :, :].rearrange("p a b -> p (a b)"), scalar=DECODE_GAIN,
                                        in1=Wh[j % RW].rearrange("p a b -> p (a b)"),
                                        op0=ALU.mult, op1=ALU.subtract).then_inc(s_ffl, 1)

            def sum_slots(b, half):
                if half == 0:
                    ve.wait_ge(s_z, 2 * b + 2)
                    if b >= 2:
                        ve.wait_ge(s_rt, b - 1)
                v_.tensor_reduce(R[:, b % 2, H * half:H * half + H],
                                 view(Z[:, b % 2], [[16 * NSLOT, H], [1, HD], [8, NSLOT]], 8 * NSLOT * half),
                                 AX.X, ALU.add).then_inc(s_r, 1)

            def poly_step(u):
                ve.wait_ge(s_sq, u + 1)
                if u >= 2:
                    ve.wait_ge(s_th, u - 1)
                v_.scalar_tensor_tensor(out=poly[:, u % 2], in0=sq[:, u % 2], scalar=GATE_K,
                                        in1=bank[2 * (u % 2)][:, :], op0=ALU.add, op1=ALU.mult).then_inc(s_poly, 1)

            def gate_up(u):
                ve.wait_ge(s_th, u + 1)
                v_.scalar_tensor_tensor(out=gel[:, u % 2], in0=th[:, u % 2], scalar=1.0,
                                        in1=bank[2 * (u % 2)][:, :], op0=ALU.add, op1=ALU.mult).then_inc(s_gel, 1)
                ve.wait_ge(s_gel, u + 1)
                ve.wait_ge(s_u, u + 1)
                if u >= 2:
                    ve.wait_ge(s_il, u - 1)
                v_.scalar_tensor_tensor(out=act[:, u % 2], in0=bank[2 * (u % 2) + 1][:, :], scalar=UP_SCALE,
                                        in1=gel[:, u % 2], op0=ALU.mult, op1=ALU.mult).then_inc(s_act, 1)

            for t in range(TICKS):
                for b in batch(t, T_SPLIT):
                    split_max(b)
                for b in batch(t, T_NORM):
                    normalise(b)
                for b in batch(t, T_LN2):
                    ve.wait_ge(s_proj, b + 1)
                    v_.tensor_tensor(X[:, b, :], X[:, b, :], bank[7][:, 0:D], ALU.add).then_inc(s_x1, 1)
                    ve.wait_ge(s_x1, b + 1)
                    ln_stats(1, b)
                for j in early_decode(t, 0):
                    codes_bits(j)
                for h in conv_heads(t):
                    if h >= KVR:
                        products(h)
                for b in batch(t, T_SUM):
                    sum_slots(b, 0)
                for b, g in group(t, T_SCORES):
                    group_max(b, g)
                for b in batch(t, T_SUM2):
                    sum_slots(b, 1)
                for b in batch(t, T_LN3):
                    ve.wait_ge(s_rt, b + 1)
                    v_.tensor_tensor(X[:, b, :], X[:, b, :], bank[6][:, 0:D], ALU.add).then_inc(s_x2, 1)
                    ve.wait_ge(s_x2, b + 1)
                    ln_stats(2, b)
                for b in batch(t, T_YT):
                    ve.wait_ge(s_yth, b + 1)
                    v_.tensor_tensor(xTl[:, :, P * b:P * b + P],
                                     bank[6][:, 0:D].rearrange("p (c t) -> p c t", c=2),
                                     xTh[:, :, P * b:P * b + P], ALU.subtract).then_inc(s_ytl, 1)
                for j in early_decode(t, 3):
                    w_lo(j)
                for u in early_units(t):
                    poly_step(u)
                    gate_up(u)
            for u in range(2 * EARLY, UNITS):
                poly_step(u)
                for j in late_decode(u, 0):
                    codes_bits(j)
                for j in late_decode(u, 3):
                    w_lo(j)
                gate_up(u)
            for b in range(B):
                if b == 0:
                    ve.wait_ge(s_down, UNITS)
                v_.scalar_tensor_tensor(out=XN[:, b, :], in0=bank[4 + b // 2][:, D * (b % 2):D * (b % 2) + D],
                                        scalar=1.0 / W_GAIN, in1=X[:, b, :],
                                        op0=ALU.mult, op1=ALU.add).then_inc(s_fin, 1)

        @block.tensor
        def _(pe):
            t_ = nc.tensor
            mmul = t_.matmul
            pe.wait_ge(s_const, 1)

            def transpose_x(g):
                for pr in range(2 * g, 2 * g + 2):
                    for b in (2 * pr, 2 * pr + 1):
                        pe.wait_ge(s_xn[0], b + 1)
                        if pr >= 2 and b % 2 == 0:
                            pe.wait_ge(s_xtl, pr - 1)
                        for c in range(2):
                            last = t_.transpose(bank[pr % 2][:, 256 * (b % 2) + P * c:256 * (b % 2) + P * c + P],
                                                XN[:, b, P * c:P * c + P], ident[:, :])
                    last.then_inc(s_xt, 1)

            def three(out, ah, al, bh, bl, chunks, **kw):
                n = 0
                for c in chunks:
                    for a, w in ((ah, bh), (ah, bl), (al, bh)):
                        ins = mmul(out, a(c), w(c), start=(n == 0), stop=(n == 3 * len(chunks) - 1))
                        n += 1
                return ins

            def project_qk(g):
                pe.wait_ge(s_xtl, 2 * g + 2)
                for n in range(4):
                    if g:
                        pe.wait_ge(s_qkl, n + 1)
                    k, m = n // 2, n % 2
                    pe.wait_ge(s_wl, k + 1)
                    three(bank[2 + n][:, :],
                          lambda c: wqkvh[:, c, k, P * m:P * m + P], lambda c: wqkvl[:, c, k, P * m:P * m + P],
                          lambda c: xTh[:, c, HALF * g:HALF * g + HALF], lambda c: xTl[:, c, HALF * g:HALF * g + HALF],
                          range(2)).then_inc(s_qk, 1)

            def project_v(g):
                for b in range(4 * g, 4 * g + 4):
                    if b == 0:
                        pe.wait_ge(s_wl, 3)
                    if b >= 2:
                        pe.wait_ge(s_vs, b - 1)
                    three(bank[6 + b % 2][:, 0:D],
                          lambda c: xTh[:, c, P * b:P * b + P], lambda c: xTl[:, c, P * b:P * b + P],
                          lambda c: wqkvh[:, c, 2, :], lambda c: wqkvl[:, c, 2, :], range(2)).then_inc(s_v, 1)

            transpose_x(0)
            project_qk(0)
            transpose_x(1)
            project_v(0)
            project_qk(1)
            project_v(1)
            pe.wait_ge(s_qkl, 8)

            reader = {6: (s_vs, B), 7: (s_vs, B)}

            def take(n, last_reader, count):
                pe.wait_ge(*reader[n])
                reader[n] = (last_reader, count)

            def convolve(h, lc):
                if h >= CONV_EARLY:
                    take(6 + lc, s_ys[lc], h + 1)
                elif h >= 2:
                    pe.wait_ge(s_ys[lc], h - 1)
                out = conv_bank(h, lc)[:, 0:320]
                if lc == 0:
                    pe.wait_ge(s_tdiag, h + 1)
                    pe.wait_ge(s_kv[0], h + 1)
                    mmul(out, T[:, h, 0:P], KV[:, h % KVR, 0, :], start=True, stop=True).then_inc(s_y[0], 1)
                else:
                    mmul(out, T[:, h, P:2 * P], KV[:, h % KVR, 0, :], start=True, stop=False)
                    pe.wait_ge(s_kv[1], h + 1)
                    mmul(out, T[:, h, 0:P], KV[:, h % KVR, 1, :], start=False, stop=True).then_inc(s_y[1], 1)

            for h in range(CONV_EARLY):
                for lc in range(2):
                    convolve(h, lc)

            def scores(b, g):
                n = 4 * b + g
                if n < 2:
                    pe.wait_ge(s_xtl, 4)
                else:
                    pe.wait_ge(s_max, n - 1)
                if n == 0:
                    pe.wait_ge(s_const, 6)
                par, pairs = head_group(g)
                out = bank[n % 2]
                mmul(out[:, :], identb[:, :], maskb[:, :, :].rearrange("p h t -> p (h t)"), start=True, stop=False,
                     skip_group_check=True)
                rows = slice(64 * par, 64 * par + 64)
                for j, pair in enumerate(pairs):
                    last = mmul(out[:, P * j:P * j + P], QK[rows, 0, pair, P * b:P * b + P],
                                QK[rows, 1, pair, P * b:P * b + P], start=False, stop=(j == 3),
                                skip_group_check=True)
                last.then_inc(s_s, 1)

            def scores_t(b, g):
                n = 4 * b + g
                if n == 0:
                    for lc in range(2):
                        pe.wait_ge(s_ys[lc], CONV_EARLY)
                if n == 0:
                    pe.wait_ge(s_sel, 1)
                if n >= 2:
                    pe.wait_ge(s_exp, n - 1)
                par, pairs = head_group(g)
                out = bank[2 + n % 2]
                rows = slice(64 * par, 64 * par + 64)
                mrows = slice(64 * par, 64 * par + 48)
                for j, pair in enumerate(pairs):
                    o = out[:, P * j:P * j + P]
                    mmul(o, sel[mrows, 4 * g + j, :], mT[mrows, b % 2, :], start=True, stop=False,
                         skip_group_check=True)
                    last = mmul(o, QK[rows, 1, pair, P * b:P * b + P], QK[rows, 0, pair, P * b:P * b + P],
                                start=False, stop=True, skip_group_check=True)
                last.then_inc(s_stt, 1)

            def attend(b, g):
                n = 4 * b + g
                pe.wait_ge(s_msk, n + 1)
                if g == 0:
                    if b == 0:
                        pe.wait_ge(s_vs, B)
                        pe.wait_ge(s_const, 9)
                    if b >= 2:
                        pe.wait_ge(s_och, 4 * (b - 2) + 2)
                for j in range(4):
                    last = mmul(bank[4 + b % 2][32 * j:32 * j + 32, P * g:P * g + P], vaug[:, b, 4 * g + j, :],
                                PT[:, n % PR, j, :], start=True, stop=True)
                last.then_inc(s_pv, 1)

            def gate_and_up(u):
                j, nib, g = ORDER[u]
                if u == 0:
                    pe.wait_ge(s_max, 4 * B)
                    pe.wait_ge(s_exp, 4 * B)
                if (j, nib) == (0, 0):
                    pe.wait_ge(s_ytl, 4 * g + 4)
                pe.wait_ge(s_ffl, j + 1)
                for w, (out, signal) in enumerate(((bank[2 * (u % 2)], s_g), (bank[2 * (u % 2) + 1], s_u))):
                    if u >= 2:
                        pe.wait_ge(s_gel if w == 0 else s_act, u - 1)
                    col = slice(256 * w + P * nib, 256 * w + P * nib + P)
                    three(out[:, :],
                          lambda c: Wh[j % RW][:, c, col], lambda c: Wl[j % RW][:, c, col],
                          lambda c: xTh[:, c, HALF * g:HALF * g + HALF],
                          lambda c: xTl[:, c, HALF * g:HALF * g + HALF], range(2)).then_inc(signal, 1)

            def down(u):
                j, nib, g = ORDER[u]
                if (j, nib) == (0, 0):
                    if g == 0:
                        pe.wait_ge(s_och, 4 * B)
                    else:
                        pe.wait_ge(s_x1, B)
                        pe.wait_ge(s_qx, 2 * B)
                        pe.wait_ge(s_ytl, B)
                pe.wait_ge(s_il, u + 1)
                for tt in range(4):
                    b = 4 * g + tt
                    out = bank[4 + b // 2][:, D * (b % 2):D * (b % 2) + D]
                    t = slice(P * tt, P * tt + P)
                    for n, (a, w) in enumerate(((ih, Wh), (ih, Wl), (il, Wh))):
                        last = mmul(out, a[:, u % IR, t], w[j % RW][:, nib, 512:768],
                                    start=((j, nib) == (0, 0) and tt % 2 == 0 and n == 0),
                                    stop=((j, nib) == (STEPS - 1, 1) and n == 2),
                                    skip_group_check=True)
                last.then_inc(s_down, 1)

            for t in range(TICKS):
                for b, g in group(t, T_SCORES):
                    if g == 0 and b % 4 == 0:
                        for k in range(2):
                            pe.wait_ge(s_pack[b // 4][k], 64)
                    scores(b, g)
                for b in batch(t, T_TOK):
                    pe.wait_ge(s_pvs, b + 1)
                    for g in range(4):
                        last = t_.transpose(bank[4 + b % 2][:, P * g:P * g + P], pvs[:, b % 2, P * g:P * g + P],
                                            ident[:, :])
                    last.then_inc(s_tok, 1)
                    take(6, s_och, 4 * b + 1)
                    mmul(bank[6][:, 0:272], later[:, :], vaug[:, b, :, 0:DH + 1],
                         start=True, stop=True).then_inc(s_suf, 1)
                for b in batch(t, T_OT):
                    take(7, s_ott, b + 1)
                    pe.wait_ge(s_och, 4 * b + 4)
                    for c in range(2):
                        last = t_.transpose(bank[7][:, P * c:P * c + P], o_sb[:, b % 2, P * c:P * c + P],
                                            ident[:, :])
                    last.then_inc(s_ot, 1)
                for b in batch(t, T_PROJ):
                    take(7, s_x1, b + 1)
                    pe.wait_ge(s_ott, b + 1)
                    if b == 0:
                        pe.wait_ge(s_w[3], 16)
                    for c in range(2):
                        last = mmul(bank[7][:, 0:D], oT[:, b % 2, c, :], wo[:, c, :], start=(c == 0), stop=(c == 1))
                    last.then_inc(s_proj, 1)
                for b in batch(t, T_QT):
                    take(7, s_qx, 2 * b + 2)
                    pe.wait_ge(s_xn[1], b + 1)
                    for c in range(2):
                        last = t_.transpose(bank[7][:, P * c:P * c + P], XN[:, b, P * c:P * c + P], ident[:, :])
                    last.then_inc(s_qt, 1)
                for b in batch(t, T_RT):
                    take(6, s_x2, b + 1)
                    pe.wait_ge(s_r, 2 * b + 2)
                    for c in range(2):
                        last = t_.transpose(bank[6][:, P * c:P * c + P],
                                            R[:, b % 2, H * c:H * c + H, :].rearrange("p h i -> p (h i)"),
                                            ident[:, :])
                    last.then_inc(s_rt, 1)
                for b in batch(t, T_YT):
                    take(6, s_ytl, b + 1)
                    pe.wait_ge(s_xn[2], b + 1)
                    for c in range(2):
                        last = t_.transpose(bank[6][:, P * c:P * c + P], XN[:, b, c::2], ident[:, :])
                    last.then_inc(s_yt, 1)
                for b, g in group(t, T_ST):
                    if g == 0:
                        pe.wait_ge(s_mt, b + 1)
                    scores_t(b, g)
                for b in batch(t, T_MPT):
                    take(7, s_mt, b + 1)
                    pe.wait_ge(s_mch, 5 * b + 5)
                    t_.transpose(bank[7][:, 0:64].bitcast(BF16)[0:112, :], mp[:, b % 2, :],
                                 identb[:, :]).then_inc(s_mpt, 1)
                for b, g in group(t, T_ATT):
                    attend(b, g)
                for h in conv_heads(t):
                    convolve(h, 0)
                for h in conv_heads(t):
                    convolve(h, 1)
                for u in early_units(t):
                    gate_and_up(u)
                    if u >= 2:
                        down(u - 2)
            for u in range(2 * EARLY, UNITS):
                gate_and_up(u)
                down(u - 2)
            down(UNITS - 2)
            down(UNITS - 1)


def kernel(x, ctx_2048, L0_attn_Wq, L0_attn_Wk, L0_attn_Wv, L0_attn_Wo, L0_xattn_ssm_kernel, L0_xattn_D,
           L0_ffn_gate_W_packed, L0_ffn_gate_scales, L0_ffn_up_W_packed, L0_ffn_up_scales,
           L0_ffn_down_W_packed, L0_ffn_down_scales):
    import numpy as np
    import concourse.bacc as bacc
    from concourse.bass_utils import run_bass_kernel_spmd

    def arr(a):
        return np.asarray(a)

    def regroup(a, axis):
        a = arr(a)
        a = np.moveaxis(a, axis, 0)
        a = a.reshape(2, 4, 2, DH, D).transpose(0, 2, 1, 3, 4).reshape(D, D)
        return np.moveaxis(a, 0, axis)

    keys = arr(ctx_2048).transpose(2, 0, 1).reshape(2, P, B, H, HD)[:, ::-1]
    keys = np.concatenate([keys, keys[..., :4]], axis=-1)

    wqkv = np.stack([arr(L0_attn_Wq), arr(L0_attn_Wk), regroup(L0_attn_Wv, 1)])
    wo = regroup(L0_attn_Wo, 0)
    kernel_rows = np.zeros((H, 384), np.float32)
    kernel_rows[:, 128:] = arr(L0_xattn_ssm_kernel)

    def by_step(rows):
        k = rows.shape[1]
        return rows.reshape(STEPS, P, 2, k).transpose(0, 3, 2, 1).reshape(STEPS, k, 2 * P)

    down_codes = arr(L0_ffn_down_W_packed).T.reshape(STEPS, P, D)
    codes = np.concatenate([by_step(arr(L0_ffn_gate_W_packed)), by_step(arr(L0_ffn_up_W_packed)), down_codes],
                           axis=2)
    gu_scale = np.concatenate([by_step(arr(L0_ffn_gate_scales)), by_step(arr(L0_ffn_up_scales))], axis=2)
    down_scale = arr(L0_ffn_down_scales).T

    nc = bacc.Bacc("TRN2", target_bir_lowering=False, num_devices=1)
    named = [("x", arr(x)), ("ctx", keys), ("wqkv", wqkv), ("wo", wo), ("ker", kernel_rows),
             ("skip", arr(L0_xattn_D)), ("gu_scale", gu_scale), ("down_scale", down_scale), ("codes", codes)]
    arrays, args = {}, []
    for name, a in named:
        a = np.ascontiguousarray(a)
        arrays[f"in_{name}"] = a
        args.append(nc.dram_tensor(f"in_{name}", a.shape, mybir.dt.from_np(a.dtype), kind="ExternalInput").ap())
    out = nc.dram_tensor("out", (B, P, D), F32, kind="ExternalOutput").ap()
    build(nc, *args, out)
    r = run_bass_kernel_spmd(nc, [arrays], core_ids=[0])
    return r.results[0]["out"]
```

```python
from contextlib import ExitStack

import concourse.bass as bass
from concourse import mybir

F32, F16, BF16, I32 = mybir.dt.float32, mybir.dt.float16, mybir.dt.bfloat16, mybir.dt.int32
ACT = mybir.ActivationFunctionType
ALU = mybir.AluOpType
AX = mybir.AxisListType

P = 128
B = 8
D = 256
CHUNKS = D // P
H = 16
DH = D // H
HD = 8
NPAIR = 5
NSLOT = 9
MLP = 2048
STEPS = MLP // D
UNITS = STEPS * 4
RW = 4
HALF = 512
EPS = 1e-5
SCALE = 1.0 / 128 ** 0.5
NEG = -1.0e30
W_GAIN = 16.0
DECODE_GAIN = 2.0 ** 14 * W_GAIN
GELU_A, GELU_B = 0.7978845608028654, 0.044715
GATE_K = W_GAIN ** 2 / GELU_B
TANH_SCALE = GELU_A * GELU_B / W_GAIN ** 3
UP_SCALE = 0.5 / W_GAIN ** 2


def build(nc, x_d, ctx_d, wqkv_d, wo_d, ker_d, skip_d, gu_scale_d, down_scale_d, codes_d, out_d):
    scr = nc.dram_tensor("qk_scratch", (2, 2, H, 3, DH, HALF), F16, kind="Internal").ap()

    ctx = ExitStack()
    with ctx:
        def sb(name, shape, dt=F32):
            return ctx.enter_context(nc.sbuf_tensor(name, shape, dt))

        def sem(name):
            return ctx.enter_context(nc.semaphore(name))

        def view(ap, dims, offset=0):
            return bass.AP(ap.tensor, ap.offset + offset, [list(ap.ap[0])] + [list(d) for d in dims])

        X = sb("X", [P, B, D])
        XN = sb("XN", [P, B, D])
        xTh = sb("xTh", [P, CHUNKS, B * P], F16)
        xTl = sb("xTl", [P, CHUNKS, B * P], F16)
        w16 = sb("w16", [P, 2, CHUNKS, 3, D], F16)
        wqkvh, wqkvl = w16[:, 0], w16[:, 1]
        W32 = w16[:, :, :, :, :].rearrange("p a b c d -> p (a b c d)").bitcast(F32).rearrange("p (n w) -> p n w", n=2)
        wo = sb("wo", [P, CHUNKS, D])
        Ys = sb("Ys", [P, H, 2, B, NPAIR * HD])
        early = Ys[:, :, :, :, :].rearrange("p a b c d -> p (a b c d)")
        wqkv32 = early[:, 4608:6144].rearrange("p (c w n) -> p c w n", c=CHUNKS, w=3)
        nat = early[:, 6144:10240].bitcast(F16).rearrange(
            "p (g k m s t) -> p g k m s t", g=2, k=2, m=2, s=2)
        STAGING_HEAD = 4096 // (2 * B * NPAIR * HD)
        arena = sb("arena", [P, 9728])
        kx = arena[:, 0:3072].rearrange("p (m b h i) -> p m b h i", m=2, b=B, h=H)
        KVR = 4
        KV = arena[:, 3072:5632].rearrange("p (r m n) -> p r m n", r=KVR, m=2)
        T = arena[:, 5632:9728].rearrange("p (h l) -> p h l", h=H)
        Z = arena[:, 0:4608].rearrange("p (r h s) -> p r h s", r=2, h=2 * H)
        codes = arena[:, 5632:7168].bitcast(I32).rearrange("p (r n) -> p r n", r=2)
        scales = arena[:, 7168:8704].rearrange("p (r n) -> p r n", r=2)
        bits = arena[:, 8704:9472].bitcast(I32)
        bits2 = arena[:, 4608:5376].bitcast(I32)
        Wa = sb("Wa", [P, 4, 2, 768], F16)
        QK = sb("QK", [P, 2, H // 2, B * P], F16)
        late = QK[:, :, :, :].rearrange("p a b c -> p (a b c)").bitcast(F32)
        sq = late[:, 0:1024].rearrange("p (r t) -> p r t", r=2)
        poly = late[:, 1024:2048].rearrange("p (r t) -> p r t", r=2)
        th = late[:, 2048:3072].rearrange("p (r t) -> p r t", r=2)
        gel = late[:, 3072:4096].rearrange("p (r t) -> p r t", r=2)
        act = late[:, 4096:5120].rearrange("p (r t) -> p r t", r=2)
        IR = 4
        ih = late[:, 5120:6144].bitcast(F16).rearrange("p (r t) -> p r t", r=IR)
        il = late[:, 6144:7168].bitcast(F16).rearrange("p (r t) -> p r t", r=IR)
        vaug = sb("vaug", [P, B, H, 32])
        Wb = vaug[:, :, :, :].rearrange("p b h d -> p (b h d)").bitcast(F16)[:, 0:6144].rearrange(
            "p (s n w) -> p s n w", s=4, n=2)
        Wh = [Wa[:, 0], Wa[:, 1], Wb[:, 0], Wb[:, 1]]
        Wl = [Wa[:, 2], Wa[:, 3], Wb[:, 2], Wb[:, 3]]
        PR = 4
        PT = sb("PT", [P, PR, 4, P])
        pvs = sb("pvs", [P, 2, 512])
        tail = sb("tail", [P, H, DH + 1])
        num = sb("num", [P, H, DH + 1])
        rec = sb("rec", [P, H])
        o_sb = sb("o_sb", [P, 2, D])
        oT = sb("oT", [P, 2, CHUNKS, P])
        qx = sb("qx", [P, 2, 2 * H, 12])
        R = sb("R", [P, 2, 2 * H, HD])
        stats = sb("stats", [P, B, 6])
        mv = sb("mv", [P, B, 2])
        veps = sb("veps", [P, B])
        shift = sb("shift", [P, B])
        rstd = sb("rstd", [P, B])
        nhalf = sb("nhalf", [P, B])
        mx = sb("mx", [P, 2, H])
        mm = sb("mm", [P, 2, H])
        res1 = sb("res1", [P, H])
        mp = sb("mp", [P, 2, 112], BF16)
        mT = sb("mT", [112, 2, P], BF16)
        em = sb("em", [P, 4, H])
        ident = sb("ident", [P, P])
        anti = sb("anti", [P, P])
        identb = sb("identb", [P, P], BF16)
        later = sb("later", [P, P])
        maskb = sb("maskb", [P, P], BF16)
        mask_t = sb("mask_t", [P, P], BF16)
        sel = sb("sel", [112, H, P], BF16)
        sel_row = sb("sel_row", [112, H], BF16)
        guard = sb("guard", [P, 1])
        skip = sb("skip", [P, H])

        bank = [ctx.enter_context(nc.psum_tensor(f"bank{i}", [P, 512], F32)) for i in range(8)]

        s_x = [sem(f"s_xin{pr}") for pr in range(4)]
        s_w = [sem(f"s_w{c}") for c in "qkvo"]
        s_skip = sem("s_skip")
        s_sel = sem("s_sel")
        s_ctx = [sem(f"s_ctx{g}") for g in range(2)]
        s_toep = [sem(f"s_toep{g}") for g in range(2)]
        s_const = sem("s_const")
        s_zero = sem("s_zero")
        s_st = [sem(f"s_st{n}") for n in range(3)]
        s_mv = [sem(f"s_mv{n}") for n in range(3)]
        s_rstd = [sem(f"s_rstd{n}") for n in range(3)]
        s_xn = [sem(f"s_xn{n}") for n in range(3)]
        s_xt = sem("s_xt")
        s_xth, s_xtl = sem("s_xth"), sem("s_xtl")
        s_wh, s_wl = sem("s_wh"), sem("s_wl")
        s_qk = sem("s_qk")
        s_qkh, s_qkl = sem("s_qkh"), sem("s_qkl")
        s_scr = [sem(f"s_scr{i}") for i in range(4)]
        s_pack = [[sem(f"s_pack{g}{k}") for k in range(2)] for g in range(2)]
        s_v, s_vs = sem("s_v"), sem("s_vs")
        s_tdiag = sem("s_tdiag")
        s_kv = [sem("s_kv0"), sem("s_kv1")]
        s_y, s_ys = [sem(f"s_y{c}") for c in range(2)], [sem(f"s_ys{c}") for c in range(2)]
        s_s, s_max = sem("s_s"), sem("s_max")
        s_mch = sem("s_mch")
        s_em = sem("s_em")
        s_mpt = sem("s_mpt")
        s_mt = sem("s_mt")
        s_stt = sem("s_stt")
        s_exp, s_pv = sem("s_exp"), sem("s_pv")
        s_pvs, s_tok, s_suf = sem("s_pvs"), sem("s_tok"), sem("s_suf")
        s_och = sem("s_och")
        s_ot, s_ott, s_proj, s_x1 = sem("s_ot"), sem("s_ott"), sem("s_proj"), sem("s_x1")
        s_qt, s_qx, s_z, s_r = sem("s_qt"), sem("s_qx"), sem("s_z"), sem("s_r")
        s_rt, s_x2 = sem("s_rt"), sem("s_x2")
        s_yt, s_yth, s_ytl = sem("s_yt"), sem("s_yth"), sem("s_ytl")
        s_code = [sem(f"s_code{r}") for r in range(2)]
        s_bits = sem("s_bits")
        s_w32, s_ffh, s_ffl = sem("s_w32"), sem("s_ffh"), sem("s_ffl")
        s_g, s_u, s_sq, s_poly, s_th = sem("s_g"), sem("s_u"), sem("s_sq"), sem("s_poly"), sem("s_th")
        s_gel, s_act, s_ih, s_il, s_down = sem("s_gel"), sem("s_act"), sem("s_ih"), sem("s_il"), sem("s_down")
        s_il_last = sem("s_il_last")
        s_fin, s_out = sem("s_fin"), sem("s_out")
        block = ctx.enter_context(nc.Block())

        (T_SCORES, T_SPLIT, T_MPT, T_ST, T_ATT, T_PVOUT, T_TOK, T_NORM, T_OT, T_PROJ, T_LN2, T_RSTD2, T_APPLY2,
         T_QT, T_MIX, T_MIX2, T_SUM, T_SUM2, T_RT, T_LN3, T_RSTD3, T_APPLY3, T_YT) = (
            0, 4, 5, 6, 8, 11, 12, 12, 14, 15, 15, 16, 17, 20, 21, 21, 23, 24, 26, 26, 27, 28, 30)
        CONV_EARLY = 6
        CONV_RATE = 1
        UNIT_TICKS = (43, 45, 48, 49, 51, 52, 57, 62)
        EARLY = len(UNIT_TICKS) // 2
        T_ZERO = 14
        DECODE = (14, 17, 37, 42)
        DECODE_AHEAD = 7

        TICKS = max(4 * (B - 1) + T_YT, UNIT_TICKS[-1],
                    DECODE[EARLY - 1] + 3) + 1

        ORDER = ([(j, n, g) for g in range(2) for j in range(EARLY) for n in range(2)]
                 + [(j, n, g) for j in range(EARLY, STEPS) for n in range(2) for g in range(2)])
        last_of = {j: u for u, (j, _, _) in enumerate(ORDER)}

        def early_units(t):
            return [u for u, tick in enumerate(UNIT_TICKS) if tick == t]

        def early_decode(t, at):
            return [j for j in range(EARLY) if DECODE[j] + at == t]

        def late_decode(u, at):
            j, rest = divmod(u - at + DECODE_AHEAD, 4)
            return [j] if rest == 0 and EARLY <= j < STEPS else []

        def batch(t, at):
            b, r = divmod(t - at, 4)
            return [b] if r == 0 and 0 <= b < B else []

        def group(t, at):
            n = t - at
            return [divmod(n, 4)] if 0 <= n < 4 * B else []

        def conv_heads(t):
            return [h for h in range(CONV_EARLY + CONV_RATE * t, CONV_EARLY + CONV_RATE * (t + 1)) if h < H]

        def conv_bank(h, lc):
            return bank[2 + (2 * h + lc) % 4] if h < CONV_EARLY else bank[6 + lc]

        def head_group(g):
            return g % 2, [4 * (g // 2) + j for j in range(4)]

        @block.sync
        def _(sp):
            def load_x(pr, n):
                sp.dma_start(X[:, 2 * pr:2 * pr + 2 * n, :],
                             x_d[2 * pr:2 * pr + 2 * n].rearrange("b t d -> t b d")).then_inc(s_x[pr], 16)

            def load_w(w):
                sp.dma_start(wqkv32[:, :, w, :],
                             wqkv_d[w].rearrange("(c p) n -> p c n", p=P)).then_inc(s_w[w], 16)

            load_x(0, 1)
            load_w(0)
            load_x(1, 1)
            load_w(1)
            load_x(2, 2)
            load_w(2)
            for m in range(2):
                sp.dma_start(kx[:, m], ctx_d[m]).then_inc(s_ctx[m], 16)
            sp.dma_start(skip[:, :], bass.AP(skip_d.tensor, skip_d.offset, [[0, P], [1, H]])).then_inc(s_skip, 16)
            for g in range(2):
                sp.dma_start(T[:, 8 * g:8 * g + 8, :],
                             bass.AP(ker_d.tensor, ker_d.offset + 1 + 8 * g * 384,
                                     [[1, P], [384, 8], [1, D]])).then_inc(s_toep[g], 16)
            sp.dma_start(wo[:, :, :], wo_d.rearrange("(c p) n -> p c n", p=P)).then_inc(s_w[3], 16)
            for g in range(2):
                for k in range(2):
                    sp.wait_ge(s_qkl, 4 * g + 2 * k + 2)
                    for m in range(2):
                        for part in range(3 if k == 0 else 2):
                            sp.dma_start(scr[g, k, 8 * m:8 * m + 8, part],
                                         nat[:, g, k, m, part % 2, :]).then_inc(s_scr[2 * g + k], 16)
                for k in range(2):
                    sp.wait_ge(s_scr[2 * g + k], 96 if k == 0 else 64)
                    for par in range(2):
                        for two in range(2):
                            first = 1 if k == 0 and two else 0
                            src = scr[g, k, par::2, first:first + 2].rearrange("h s d t -> (s d) h t")
                            rows = 64 * par + 32 * two
                            sp.dma_start(QK[rows:rows + 32, k, :, HALF * g:HALF * g + HALF],
                                         src).then_inc(s_pack[g][k], 16)

            def load_codes(j):
                r = j % 2
                if j == 0:
                    for lc in range(2):
                        sp.wait_ge(s_y[lc], H)
                if j >= 2:
                    sp.wait_ge(s_w32, 2 * (j - 1))
                sp.dma_start(codes[:, r, :], codes_d[j]).then_inc(s_code[r], 16)
                sp.dma_start(scales[:, r, 0:512], bass.AP(
                    gu_scale_d.tensor, gu_scale_d.offset + j * 8 * 512,
                    [[512, 8], [0, 16], [1, 512]])).then_inc(s_code[r], 16)
                sp.dma_start(scales[:, r, 512:768], bass.AP(
                    down_scale_d.tensor, down_scale_d.offset + j * 8 * D,
                    [[D, 8], [0, 16], [1, D]])).then_inc(s_code[r], 16)

            for j in range(STEPS):
                load_codes(j)
            for b in range(0, B, 2):
                sp.wait_ge(s_fin, b + 2)
                sp.dma_start(out_d[b:b + 2].rearrange("b t d -> t b d"), XN[:, b:b + 2, :]).then_inc(s_out, 16)
            sp.wait_ge(s_out, 16 * B // 2)

        @block.gpsimd
        def _(pool):
            g_ = nc.gpsimd
            z = [0]

            def own(ins):
                z[0] += 1
                ins.then_inc(s_zero, 1)
                pool.wait_ge(s_zero, z[0])

            own(g_.memset(ident[:, :], 0.0))
            g_.affine_select(out=ident[:, :], in_=ident[:, :], compare_op=ALU.not_equal, fill=1.0, base=0,
                             pattern=[[-1, P]], channel_multiplier=1).then_inc(s_const, 1)
            own(g_.memset(anti[:, :], 0.0))
            g_.affine_select(out=anti[:, :], in_=anti[:, :], compare_op=ALU.not_equal, fill=1.0,
                             base=-(P - 1), pattern=[[1, P]], channel_multiplier=1).then_inc(s_const, 1)
            own(g_.memset(nhalf[:, :], -0.5))

            def rstds(ln, n0, n):
                own(g_.tensor_scalar(veps[:, n0:n0 + n], mv[:, n0:n0 + n, 1], EPS, None, ALU.add))
                if ln == 0:
                    g_.tensor_tensor(rstd[:, n0:n0 + n], veps[:, n0:n0 + n], nhalf[:, n0:n0 + n],
                                     ALU.pow).then_inc(s_rstd[ln], n)
                else:
                    own(g_.tensor_tensor(rstd[:, n0:n0 + n], veps[:, n0:n0 + n], nhalf[:, n0:n0 + n], ALU.pow))
                    g_.tensor_scalar(shift[:, n0:n0 + 1], mv[:, n0:n0 + 1, 0], rstd[:, n0:n0 + 1], -1.0,
                                     ALU.mult, ALU.mult).then_inc(s_rstd[ln], 1)

            for n0, n in ((0, 2), (2, 2), (4, 4)):
                pool.wait_ge(s_mv[0], n0 + n)
                rstds(0, n0, n)
                if n0 == 2:
                    g_.memset(vaug[:, :, :, DH:DH + 1], 1.0).then_inc(s_const, 1)
                    g_.memset(vaug[:, :, :, DH + 1:32], 0.0).then_inc(s_const, 1)
            for m, sign in ((maskb, 1), (mask_t, -1)):
                own(g_.memset(m[:, :], 0.0))
                own(g_.affine_select(out=m[:, :], in_=m[:, :], compare_op=ALU.is_ge, fill=NEG, base=0,
                                     pattern=[[-sign, P]], channel_multiplier=sign))
            g_.memset(mp[:, 0, 48:64], 0.0).then_inc(s_const, 1)
            own(g_.memset(identb[:, :], 0.0))
            g_.affine_select(out=identb[:, :], in_=identb[:, :], compare_op=ALU.not_equal, fill=1.0, base=0,
                             pattern=[[-1, P]], channel_multiplier=1).then_inc(s_const, 1)

            def products(h):
                m = 1
                if h >= KVR:
                    for lc in range(2):
                        pool.wait_ge(s_y[lc], h - KVR + 1)
                a = kx[:, m, :, h, :]
                g_.tensor_tensor(
                    view(KV[:, h % KVR, m, :], [[40, B], [8, NPAIR], [1, HD]]),
                    view(a, [[12 * H, B], [0, NPAIR], [1, HD]]),
                    view(a, [[12 * H, B], [1, NPAIR], [1, HD]]), ALU.mult).then_inc(s_kv[1], 1)

            pool.wait_ge(s_ctx[1], 16)
            for h in range(KVR):
                products(h)

            own(g_.memset(later[:, :], 1.0))
            g_.affine_select(out=later[:, :], in_=later[:, :], compare_op=ALU.is_gt, fill=0.0, base=0,
                             pattern=[[-1, P]], channel_multiplier=1).then_inc(s_const, 1)
            own(g_.memset(guard[:, :], 0.0))
            own(g_.affine_select(out=guard[:, :], in_=guard[:, :], compare_op=ALU.not_equal, fill=NEG,
                                 base=-(P - 1), pattern=[[0, 1]], channel_multiplier=1))
            own(g_.memset(sel_row[:, :], 0.0))
            for first in (0, 16, 32, 64, 80, 96):
                own(g_.affine_select(out=sel_row[:, :], in_=sel_row[:, :], compare_op=ALU.not_equal, fill=-1.0,
                                     base=-first, pattern=[[-1, H]], channel_multiplier=1))
            g_.memset(mp[:, 1, 48:64], 0.0).then_inc(s_const, 1)

            def split_max(b):
                r = b % 2
                pool.wait_ge(s_max, 4 * b + 4)
                if b >= 2:
                    pool.wait_ge(s_em, b - 1)
                g_.tensor_scalar(mm[:, r, :], mx[:, r, :], guard[:, 0:1], None, ALU.max).then_inc(s_mch, 1)
                pool.wait_ge(s_mch, 5 * b + 1)
                if b >= 2:
                    pool.wait_ge(s_mpt, b - 1)

                def twice(part):
                    return view(mp[:, r, :], [[64, 2], [1, H]], 16 * part)

                def rep(t):
                    return view(t, [[0, 2], [1, H]])

                g_.tensor_copy(twice(0), rep(mm[:, r, :])).then_inc(s_mch, 1)
                pool.wait_ge(s_mch, 5 * b + 2)
                g_.tensor_tensor(res1[:, :], mm[:, r, :], mp[:, r, 0:16], ALU.subtract).then_inc(s_mch, 1)
                pool.wait_ge(s_mch, 5 * b + 3)
                g_.tensor_copy(twice(1), rep(res1[:, :])).then_inc(s_mch, 1)
                pool.wait_ge(s_mch, 5 * b + 4)
                g_.tensor_tensor(twice(2), rep(res1[:, :]), rep(mp[:, r, 16:32]),
                                 ALU.subtract).then_inc(s_mch, 1)

            def conv_products(b, lc):
                r = b % 2
                if lc == 0:
                    pool.wait_ge(s_qx, 2 * b + 2)
                    if b >= 2:
                        pool.wait_ge(s_r, 2 * (b - 1))
                if b == 0:
                    pool.wait_ge(s_ys[lc], H)
                slots, convolved, q = 8 * NSLOT * lc, 40 * (B * lc + b), 12 * lc
                g_.tensor_tensor(view(Z[:, r], [[16 * NSLOT, H], [8, NPAIR], [1, HD]], slots),
                                 view(early, [[80 * B, H], [8, NPAIR], [1, HD]], convolved),
                                 view(qx[:, r], [[24, H], [1, NPAIR], [1, HD]], q), ALU.mult).then_inc(s_z, 1)
                g_.tensor_tensor(view(Z[:, r], [[16 * NSLOT, H], [HD + 1, 3], [1, HD]], slots + 8 * NPAIR + 1),
                                 view(early, [[80 * B, H], [8, 3], [1, HD]], convolved + 8),
                                 view(qx[:, r], [[24, H], [0, 3], [1, HD]], q), ALU.mult).then_inc(s_z, 1)

            def decode_scale(j, nib):
                if nib == 0:
                    pool.wait_ge(s_bits, 4 * j + 4)
                    pool.wait_ge(s_code[j % 2], 48 * (j // 2 + 1))
                    if j == 0:
                        pool.wait_ge(s_v, B)
                    else:
                        pool.wait_ge(s_ffl, j)
                g_.tensor_tensor(W32[:, nib, :], view(bits[:, :].bitcast(F16), [[2, 768]], nib),
                                 scales[:, j % 2, :], ALU.mult).then_inc(s_w32, 1)

            def act_lo(u):
                pool.wait_ge(s_ih, u + 1)
                if u >= IR:
                    pool.wait_ge(s_down, u - IR + 1)
                g_.tensor_tensor(il[:, u % IR], act[:, u % 2], ih[:, u % IR], ALU.subtract).then_inc(s_il, 1)

            for h in range(KVR, CONV_EARLY + CONV_RATE):
                products(h)
            for t in range(TICKS):
                for h in conv_heads(t + 1):
                    if h >= KVR:
                        products(h)
                for b in batch(t, T_MIX):
                    conv_products(b, 0)
                for j in early_decode(t, 2):
                    decode_scale(j, 1)
                for b in batch(t, T_SPLIT):
                    split_max(b)
                if t == T_ZERO:
                    for lc in range(2):
                        pool.wait_ge(s_y[lc], H)
                    own(g_.memset(Z, 0.0))
                for b in batch(t, T_RSTD3):
                    pool.wait_ge(s_mv[2], b + 1)
                    rstds(2, b, 1)
                for u in early_units(t):
                    if u >= 1:
                        act_lo(u - 1)
                for j in early_decode(t, 1):
                    decode_scale(j, 0)
                for b in batch(t, T_RSTD2):
                    pool.wait_ge(s_mv[1], b + 1)
                    rstds(1, b, 1)
                for b in batch(t, T_MIX2):
                    conv_products(b, 1)
            for u in range(2 * EARLY - 1, UNITS - 1):
                for nib in range(2):
                    for j in late_decode(u, 1 + nib):
                        decode_scale(j, nib)
                act_lo(u)

        @block.scalar
        def _(sc):
            s_ = nc.scalar

            def weight_hi(w):
                sc.wait_ge(s_w[w], 16)
                s_.activation(wqkvh[:, :, w, :], wqkv32[:, :, w, :], ACT.Copy).then_inc(s_wh, 1)

            def x_hi(g):
                for pr in range(2 * g, 2 * g + 2):
                    sc.wait_ge(s_xt, pr + 1)
                    s_.activation(xTh[:, :, 256 * pr:256 * pr + 256].rearrange("p c (b t) -> p b c t", b=2),
                                  bank[pr % 2][:, :].rearrange("p (b c t) -> p b c t", b=2, c=2),
                                  ACT.Copy).then_inc(s_xth, 1)

            def q_hi(g):
                for n in range(4):
                    sc.wait_ge(s_qk, 4 * g + n + 1)
                    s_.activation(nat[:, g, n // 2, n % 2, 0, :], bank[2 + n][:, :],
                                  ACT.Copy).then_inc(s_qkh, 1)

            def v_out(g):
                for b in range(4 * g, 4 * g + 4):
                    sc.wait_ge(s_v, b + 1)
                    s_.activation(vaug[:, b, :, 0:DH],
                                  bank[6 + b % 2][:, 0:D].rearrange("p (h d) -> p h d", h=H),
                                  ACT.Copy).then_inc(s_vs, 1)

            weight_hi(0)
            weight_hi(1)
            x_hi(0)
            weight_hi(2)
            q_hi(0)
            x_hi(1)
            v_out(0)
            q_hi(1)
            v_out(1)
            sc.wait_ge(s_const, 8)
            s_.activation(sel[:, :, :], view(sel_row[:, :], [[1, H], [0, P]]), ACT.Copy).then_inc(s_sel, 1)

            def conv_out(h, lc):
                if h == STAGING_HEAD and lc == 0:
                    sc.wait_ge(s_wl, 3)
                    for g in range(2):
                        for k in range(2):
                            sc.wait_ge(s_scr[2 * g + k], 96 if k == 0 else 64)
                sc.wait_ge(s_y[lc], h + 1)
                s_.activation(Ys[:, h, lc],
                              conv_bank(h, lc)[:, 0:320].rearrange("p (b k) -> p b k", b=B),
                              ACT.Copy).then_inc(s_ys[lc], 1)

            def exp_max(b):
                sc.wait_ge(s_mch, 5 * b + 1)
                if b >= 4:
                    sc.wait_ge(s_och, 4 * (b - 4) + 1)
                s_.activation(em[:, b % 4, :], mm[:, b % 2, :], ACT.Exp, scale=-SCALE).then_inc(s_em, 1)

            def probs(b, g):
                n = 4 * b + g
                sc.wait_ge(s_stt, n + 1)
                if n >= PR:
                    sc.wait_ge(s_pv, n - PR + 1)
                s_.activation(PT[:, n % PR].rearrange("p a b -> p (a b)"), bank[2 + n % 2][:, :],
                              ACT.Exp, scale=SCALE).then_inc(s_exp, 1)

            def pv_out(b):
                sc.wait_ge(s_pv, 4 * b + 4)
                if b >= 2:
                    sc.wait_ge(s_tok, b - 1)
                s_.activation(pvs[:, b % 2, :], bank[4 + b % 2][:, :], ACT.Copy).then_inc(s_pvs, 1)

            def w_hi_step(j):
                sc.wait_ge(s_w32, 2 * (j + 1))
                if j == 2:
                    sc.wait_ge(s_suf, B)
                    sc.wait_ge(s_pv, 4 * B)
                if j >= RW:
                    sc.wait_ge(s_down, last_of[j - RW] + 1)
                s_.activation(Wh[j % RW], W32[:, :, :], ACT.Copy, scale=DECODE_GAIN).then_inc(s_ffh, 1)

            def act_hi(u):
                sc.wait_ge(s_act, u + 1)
                if u >= IR:
                    sc.wait_ge(s_down, u - IR + 1)
                s_.activation(ih[:, u % IR], act[:, u % 2], ACT.Copy).then_inc(s_ih, 1)

            def unit(u):
                sc.wait_ge(s_g, u + 1)
                if u >= 2:
                    sc.wait_ge(s_poly, u - 1)
                s_.activation(sq[:, u % 2], bank[2 * (u % 2)][:, :], ACT.Square).then_inc(s_sq, 1)
                if u >= 1:
                    act_hi(u - 1)
                sc.wait_ge(s_poly, u + 1)
                if u >= 2:
                    sc.wait_ge(s_gel, u - 1)
                s_.activation(th[:, u % 2], poly[:, u % 2], ACT.Tanh, scale=TANH_SCALE).then_inc(s_th, 1)

            def ln_apply(ln, b):
                sc.wait_ge(s_x1 if ln == 1 else s_x2, b + 1)
                sc.wait_ge(s_rstd[ln], b + 1)
                s_.activation(XN[:, b, :], X[:, b, :], ACT.Identity, bias=shift[:, b:b + 1],
                              scale=rstd[:, b:b + 1]).then_inc(s_xn[ln], 1)

            for h in range(CONV_EARLY):
                for lc in range(2):
                    conv_out(h, lc)
            for t in range(TICKS):
                for b in batch(t, T_LN3):
                    sc.wait_ge(s_rt, b + 1)
                    s_.activation(X[:, b, :], bank[6][:, 0:D], ACT.Copy).then_inc(s_x2, 1)
                for b in batch(t, T_QT):
                    sc.wait_ge(s_qt, b + 1)
                    if b >= 2:
                        sc.wait_ge(s_z, 4 * (b - 2) + 4)
                    s_.activation(view(qx[:, b % 2], [[12, 2], [24, H], [1, 4]], 8),
                                  view(bank[7][:, :], [[P, 2], [8, H], [1, 4]]),
                                  ACT.Copy).then_inc(s_qx, 1)
                    s_.activation(view(qx[:, b % 2], [[12, 2], [24, H], [1, HD]]),
                                  view(bank[7][:, :], [[P, 2], [8, H], [1, HD]]),
                                  ACT.Copy).then_inc(s_qx, 1)
                for h in conv_heads(t):
                    conv_out(h, 0)
                for h in conv_heads(t):
                    conv_out(h, 1)
                for u in early_units(t):
                    unit(u)
                for b in batch(t, T_MPT):
                    exp_max(b)
                    sc.wait_ge(s_mpt, b + 1)
                    if b >= 2:
                        sc.wait_ge(s_stt, 4 * (b - 2) + 4)
                    s_.activation(mT[:, b % 2, :], bank[7][:, 0:64].bitcast(BF16)[0:112, :],
                                  ACT.Copy).then_inc(s_mt, 1)
                for b in batch(t, T_OT):
                    sc.wait_ge(s_ot, b + 1)
                    if b >= 2:
                        sc.wait_ge(s_proj, b - 1)
                    s_.activation(oT[:, b % 2], bank[7][:, 0:D].rearrange("p (c t) -> p c t", c=2),
                                  ACT.Copy).then_inc(s_ott, 1)
                for b in batch(t, T_YT):
                    sc.wait_ge(s_yt, b + 1)
                    s_.activation(xTh[:, :, P * b:P * b + P],
                                  bank[6][:, 0:D].rearrange("p (c t) -> p c t", c=2),
                                  ACT.Copy).then_inc(s_yth, 1)
                for b in batch(t, T_APPLY3):
                    ln_apply(2, b)
                for b in batch(t, T_APPLY2):
                    ln_apply(1, b)
                for b, g in group(t, T_ST):
                    probs(b, g)
                for b in batch(t, T_PVOUT):
                    pv_out(b)
                for j in early_decode(t, 2):
                    w_hi_step(j)
            for u in range(2 * EARLY, UNITS):
                unit(u)
                for j in late_decode(u, 3):
                    w_hi_step(j)
            act_hi(UNITS - 1)

        @block.vector
        def _(ve):
            v_ = nc.vector

            def ln_stats(ln, b):
                v_.bn_stats(out=stats[:, b, :], in_=X[:, b, :]).then_inc(s_st[ln], 1)
                ve.wait_ge(s_st[ln], b + 1)
                v_.bn_aggr(out=mv[:, b, :], in_=stats[:, b, :]).then_inc(s_mv[ln], 1)

            def ln_apply(ln, b, n):
                ve.wait_ge(s_rstd[ln], n)
                v_.tensor_scalar(XN[:, b, :], X[:, b, :], mv[:, b, 0:1], rstd[:, b:b + 1],
                                 ALU.subtract, ALU.mult).then_inc(s_xn[ln], 1)

            def x_lo(pr):
                ve.wait_ge(s_xth, pr + 1)
                v_.tensor_tensor(xTl[:, :, 256 * pr:256 * pr + 256].rearrange("p c (b t) -> p b c t", b=2),
                                 bank[pr % 2][:, :].rearrange("p (b c t) -> p b c t", b=2, c=2),
                                 xTh[:, :, 256 * pr:256 * pr + 256].rearrange("p c (b t) -> p b c t", b=2),
                                 ALU.subtract).then_inc(s_xtl, 1)

            def weight_lo(w):
                ve.wait_ge(s_wh, w + 1)
                v_.tensor_tensor(wqkvl[:, :, w, :], wqkv32[:, :, w, :], wqkvh[:, :, w, :],
                                 ALU.subtract).then_inc(s_wl, 1)

            for b in range(4):
                if b % 2 == 0:
                    ve.wait_ge(s_x[b // 2], 16)
                ln_stats(0, b)
            for pr in range(2):
                for b in (2 * pr, 2 * pr + 1):
                    ln_apply(0, b, 2 * pr + 2)
                weight_lo(pr)
            x_lo(0)
            x_lo(1)
            ve.wait_ge(s_x[2], 16)
            for b in range(4, B):
                ln_stats(0, b)
            weight_lo(2)
            for b in range(4, B):
                ln_apply(0, b, B)

            def q_lo(g):
                for n in range(4):
                    ve.wait_ge(s_qkh, 4 * g + n + 1)
                    v_.tensor_tensor(nat[:, g, n // 2, n % 2, 1, :], bank[2 + n][:, :],
                                     nat[:, g, n // 2, n % 2, 0, :], ALU.subtract).then_inc(s_qkl, 1)

            def products(h):
                if h == 0:
                    ve.wait_ge(s_ctx[0], 16)
                if h >= KVR:
                    for lc in range(2):
                        ve.wait_ge(s_y[lc], h - KVR + 1)
                a = kx[:, 0, :, h, :]
                v_.tensor_tensor(view(KV[:, h % KVR, 0, :], [[40, B], [8, NPAIR], [1, HD]]),
                                 view(a, [[12 * H, B], [0, NPAIR], [1, HD]]),
                                 view(a, [[12 * H, B], [1, NPAIR], [1, HD]]), ALU.mult).then_inc(s_kv[0], 1)

            def skip_tap(h):
                if h == 0:
                    ve.wait_ge(s_skip, 16)
                    ve.wait_ge(s_const, 2)
                if h % 8 == 0:
                    ve.wait_ge(s_toep[h // 8], 16)
                v_.scalar_tensor_tensor(out=T[:, h, 0:P], in0=anti[:, :], scalar=skip[:, h:h + 1],
                                        in1=T[:, h, 0:P], op0=ALU.mult, op1=ALU.add).then_inc(s_tdiag, 1)

            q_lo(0)
            x_lo(2)
            x_lo(3)
            for h in range(KVR):
                products(h)
            for h in range(8):
                skip_tap(h)
            q_lo(1)
            for h in range(8, H):
                skip_tap(h)
            for h in range(KVR, CONV_EARLY + CONV_RATE):
                products(h)

            def group_max(b, g):
                n = 4 * b + g
                if g == 0 and b >= 2:
                    ve.wait_ge(s_mch, 5 * (b - 2) + 1)
                ve.wait_ge(s_s, n + 1)
                v_.tensor_reduce(mx[:, b % 2, 4 * g:4 * g + 4],
                                 bank[n % 2][:, :].rearrange("p (h t) -> p h t", h=4),
                                 AX.X, ALU.max).then_inc(s_max, 1)

            def normalise(b):
                ve.wait_ge(s_suf, b + 1)
                ve.wait_ge(s_em, b + 1)
                v_.tensor_tensor(tail[:, :, :], bank[6][:, 0:272].rearrange("p (h d) -> p h d", h=H),
                                 view(em[:, b % 4, :], [[1, H], [0, DH + 1]]), ALU.mult).then_inc(s_och, 1)
                ve.wait_ge(s_och, 4 * b + 1)
                ve.wait_ge(s_tok, b + 1)
                v_.tensor_tensor(num[:, :, :], tail[:, :, :], view(bank[4 + b % 2][:, :], [[32, H], [1, DH + 1]]),
                                 ALU.add).then_inc(s_och, 1)
                ve.wait_ge(s_och, 4 * b + 2)
                v_.reciprocal(rec[:, :], num[:, :, DH]).then_inc(s_och, 1)
                ve.wait_ge(s_och, 4 * b + 3)
                v_.tensor_tensor(o_sb[:, b % 2, :].rearrange("p (h d) -> p h d", h=H), num[:, :, 0:DH],
                                 view(rec[:, :], [[1, H], [0, DH]]), ALU.mult).then_inc(s_och, 1)

            def codes_split(j):
                r = j % 2
                ve.wait_ge(s_code[r], 48 * (j // 2 + 1))
                v_.scalar_tensor_tensor(out=bits2[:, :], in0=codes[:, r, :], scalar=12, in1=codes[:, r, :],
                                        op0=ALU.logical_shift_left, op1=ALU.bitwise_or).then_inc(s_bits, 1)
                ve.wait_ge(s_bits, 4 * j + 1)
                if j >= 1:
                    ve.wait_ge(s_w32, 2 * j)
                v_.tensor_scalar(codes[:, r, :], bits2[:, :], 0x00070007, 9, ALU.bitwise_and,
                                 ALU.logical_shift_left).then_inc(s_bits, 1)

            def codes_join(j):
                r = j % 2
                v_.tensor_scalar(bits[:, :], bits2[:, :], 0x00080008, 12, ALU.bitwise_and,
                                 ALU.logical_shift_left).then_inc(s_bits, 1)
                ve.wait_ge(s_bits, 4 * j + 3)
                v_.tensor_tensor(bits[:, :], bits[:, :], codes[:, r, :], ALU.bitwise_or).then_inc(s_bits, 1)

            def w_lo(j):
                ve.wait_ge(s_ffh, j + 1)
                v_.scalar_tensor_tensor(out=Wl[j % RW].rearrange("p a b -> p (a b)"),
                                        in0=W32[:, :, :].rearrange("p a b -> p (a b)"), scalar=DECODE_GAIN,
                                        in1=Wh[j % RW].rearrange("p a b -> p (a b)"),
                                        op0=ALU.mult, op1=ALU.subtract).then_inc(s_ffl, 1)

            def sum_slots(b, half):
                ve.wait_ge(s_z, 4 * b + 2 * half + 2)
                if half == 0 and b >= 2:
                    ve.wait_ge(s_rt, b - 1)
                v_.tensor_reduce(R[:, b % 2, H * half:H * half + H],
                                 view(Z[:, b % 2], [[16 * NSLOT, H], [1, HD], [8, NSLOT]], 8 * NSLOT * half),
                                 AX.X, ALU.add).then_inc(s_r, 1)

            def poly_step(u):
                ve.wait_ge(s_sq, u + 1)
                if u >= 2:
                    ve.wait_ge(s_th, u - 1)
                v_.scalar_tensor_tensor(out=poly[:, u % 2], in0=sq[:, u % 2], scalar=GATE_K,
                                        in1=bank[2 * (u % 2)][:, :], op0=ALU.add, op1=ALU.mult).then_inc(s_poly, 1)

            def gate_up(u):
                ve.wait_ge(s_th, u + 1)
                v_.scalar_tensor_tensor(out=gel[:, u % 2], in0=th[:, u % 2], scalar=1.0,
                                        in1=bank[2 * (u % 2)][:, :], op0=ALU.add, op1=ALU.mult).then_inc(s_gel, 1)
                ve.wait_ge(s_gel, u + 1)
                ve.wait_ge(s_u, u + 1)
                if u >= 2:
                    ve.wait_ge(s_il, u - 1)
                v_.scalar_tensor_tensor(out=act[:, u % 2], in0=bank[2 * (u % 2) + 1][:, :], scalar=UP_SCALE,
                                        in1=gel[:, u % 2], op0=ALU.mult, op1=ALU.mult).then_inc(s_act, 1)

            for t in range(TICKS):
                for h in conv_heads(t + 1):
                    if h >= KVR:
                        products(h)
                for b, g in group(t, T_SCORES):
                    group_max(b, g)
                for b in batch(t, T_LN3):
                    ve.wait_ge(s_x2, b + 1)
                    ln_stats(2, b)
                for b in batch(t, T_YT):
                    ve.wait_ge(s_yth, b + 1)
                    v_.tensor_tensor(xTl[:, :, P * b:P * b + P],
                                     bank[6][:, 0:D].rearrange("p (c t) -> p c t", c=2),
                                     xTh[:, :, P * b:P * b + P], ALU.subtract).then_inc(s_ytl, 1)
                for b in batch(t, T_SUM2):
                    sum_slots(b, 1)
                for b in batch(t, T_SUM):
                    sum_slots(b, 0)
                for b in batch(t, T_NORM):
                    normalise(b)
                for b in batch(t, T_LN2):
                    ve.wait_ge(s_proj, b + 1)
                    v_.tensor_tensor(X[:, b, :], X[:, b, :], bank[7][:, 0:D], ALU.add).then_inc(s_x1, 1)
                    ve.wait_ge(s_x1, b + 1)
                    ln_stats(1, b)
                for u in early_units(t):
                    poly_step(u)
                    gate_up(u)
                for j in early_decode(t, 0):
                    codes_split(j)
                    codes_join(j)
                for j in early_decode(t, 3):
                    w_lo(j)
            for u in range(2 * EARLY, UNITS):
                poly_step(u)
                for j in late_decode(u, 0):
                    codes_split(j)
                for j in late_decode(u, 1):
                    codes_join(j)
                for j in late_decode(u, 4):
                    w_lo(j)
                gate_up(u)
            ve.wait_ge(s_ih, UNITS)
            v_.tensor_tensor(il[:, (UNITS - 1) % IR], act[:, (UNITS - 1) % 2], ih[:, (UNITS - 1) % IR],
                             ALU.subtract).then_inc(s_il_last, 1)
            for b in range(B):
                if b in (0, 4, 6):
                    ve.wait_ge(s_down, UNITS - 1 + b // 4 + b // 6)
                v_.scalar_tensor_tensor(out=XN[:, b, :], in0=bank[4 + b // 2][:, D * (b % 2):D * (b % 2) + D],
                                        scalar=1.0 / W_GAIN, in1=X[:, b, :],
                                        op0=ALU.mult, op1=ALU.add).then_inc(s_fin, 1)

        @block.tensor
        def _(pe):
            t_ = nc.tensor
            mmul = t_.matmul
            pe.wait_ge(s_const, 1)

            def transpose_x(g):
                for pr in range(2 * g, 2 * g + 2):
                    for b in (2 * pr, 2 * pr + 1):
                        pe.wait_ge(s_xn[0], b + 1)
                        if pr >= 2 and b % 2 == 0:
                            pe.wait_ge(s_xtl, pr - 1)
                        for c in range(2):
                            last = t_.transpose(bank[pr % 2][:, 256 * (b % 2) + P * c:256 * (b % 2) + P * c + P],
                                                XN[:, b, P * c:P * c + P], ident[:, :])
                    last.then_inc(s_xt, 1)

            def three(out, ah, al, bh, bl, chunks):
                n = 0
                for c in chunks:
                    for a, w in ((ah, bh), (ah, bl), (al, bh)):
                        ins = mmul(out, a(c), w(c), start=(n == 0), stop=(n == 3 * len(chunks) - 1))
                        n += 1
                return ins

            def project_qk(g):
                pe.wait_ge(s_xtl, 2 * g + 2)
                for n in range(4):
                    if g:
                        pe.wait_ge(s_qkl, n + 1)
                    k, m = n // 2, n % 2
                    pe.wait_ge(s_wl, k + 1)
                    three(bank[2 + n][:, :],
                          lambda c: wqkvh[:, c, k, P * m:P * m + P], lambda c: wqkvl[:, c, k, P * m:P * m + P],
                          lambda c: xTh[:, c, HALF * g:HALF * g + HALF], lambda c: xTl[:, c, HALF * g:HALF * g + HALF],
                          range(2)).then_inc(s_qk, 1)

            def project_v(g):
                for b in range(4 * g, 4 * g + 4):
                    if b == 0:
                        pe.wait_ge(s_wl, 3)
                    if b >= 2:
                        pe.wait_ge(s_vs, b - 1)
                    three(bank[6 + b % 2][:, 0:D],
                          lambda c: xTh[:, c, P * b:P * b + P], lambda c: xTl[:, c, P * b:P * b + P],
                          lambda c: wqkvh[:, c, 2, :], lambda c: wqkvl[:, c, 2, :], range(2)).then_inc(s_v, 1)

            transpose_x(0)
            project_qk(0)
            transpose_x(1)
            project_v(0)
            project_qk(1)
            project_v(1)
            pe.wait_ge(s_qkl, 8)

            reader = {6: (s_vs, B), 7: (s_vs, B)}

            def take(n, last_reader, count):
                pe.wait_ge(*reader[n])
                reader[n] = (last_reader, count)

            def convolve(h, lc):
                if h >= CONV_EARLY:
                    take(6 + lc, s_ys[lc], h + 1)
                elif h >= 2:
                    pe.wait_ge(s_ys[lc], h - 1)
                out = conv_bank(h, lc)[:, 0:320]
                if lc == 0:
                    pe.wait_ge(s_tdiag, h + 1)
                    pe.wait_ge(s_kv[0], h + 1)
                    mmul(out, T[:, h, 0:P], KV[:, h % KVR, 0, :], start=True, stop=True).then_inc(s_y[0], 1)
                else:
                    mmul(out, T[:, h, P:2 * P], KV[:, h % KVR, 0, :], start=True, stop=False)
                    pe.wait_ge(s_kv[1], h + 1)
                    mmul(out, T[:, h, 0:P], KV[:, h % KVR, 1, :], start=False, stop=True).then_inc(s_y[1], 1)

            for h in range(CONV_EARLY):
                for lc in range(2):
                    convolve(h, lc)

            def scores(b, g):
                n = 4 * b + g
                if n < 2:
                    pe.wait_ge(s_xtl, 4)
                else:
                    pe.wait_ge(s_max, n - 1)
                if n == 0:
                    pe.wait_ge(s_const, 6)
                par, pairs = head_group(g)
                out = bank[n % 2]
                mmul(out[:, :], identb[:, :], view(maskb[:, :], [[0, 4], [1, P]]), start=True, stop=False,
                     skip_group_check=True)
                rows = slice(64 * par, 64 * par + 64)
                for j, pair in enumerate(pairs):
                    last = mmul(out[:, P * j:P * j + P], QK[rows, 0, pair, P * b:P * b + P],
                                QK[rows, 1, pair, P * b:P * b + P], start=False, stop=(j == 3),
                                skip_group_check=True)
                last.then_inc(s_s, 1)

            def scores_t(b, g):
                n = 4 * b + g
                if n == 0:
                    for lc in range(2):
                        pe.wait_ge(s_ys[lc], CONV_EARLY)
                    pe.wait_ge(s_sel, 1)
                if n >= 2:
                    pe.wait_ge(s_exp, n - 1)
                par, pairs = head_group(g)
                out = bank[2 + n % 2]
                rows = slice(64 * par, 64 * par + 64)
                mrows = slice(64 * par, 64 * par + 48)
                mmul(out[:, :], identb[:, :], view(mask_t[:, :], [[0, 4], [1, P]]), start=True, stop=False,
                     skip_group_check=True)
                for j, pair in enumerate(pairs):
                    o = out[:, P * j:P * j + P]
                    mmul(o, sel[mrows, 4 * g + j, :], mT[mrows, b % 2, :], start=False, stop=False,
                         skip_group_check=True)
                    last = mmul(o, QK[rows, 1, pair, P * b:P * b + P], QK[rows, 0, pair, P * b:P * b + P],
                                start=False, stop=(j == 3), skip_group_check=True)
                last.then_inc(s_stt, 1)

            def attend(b, g):
                n = 4 * b + g
                pe.wait_ge(s_exp, n + 1)
                if g == 0:
                    if b == 0:
                        pe.wait_ge(s_vs, B)
                        pe.wait_ge(s_const, 8)
                    if b >= 2:
                        pe.wait_ge(s_och, 4 * (b - 2) + 2)
                for j in range(4):
                    last = mmul(bank[4 + b % 2][32 * j:32 * j + 32, P * g:P * g + P], vaug[:, b, 4 * g + j, :],
                                PT[:, n % PR, j, :], start=True, stop=True)
                last.then_inc(s_pv, 1)

            def gate_and_up(u):
                j, nib, g = ORDER[u]
                if u == 0:
                    pe.wait_ge(s_max, 4 * B)
                    pe.wait_ge(s_exp, 4 * B)
                if (j, nib) == (0, 0):
                    pe.wait_ge(s_ytl, 4 * g + 4)
                pe.wait_ge(s_ffl, j + 1)
                for w, (out, signal) in enumerate(((bank[2 * (u % 2)], s_g), (bank[2 * (u % 2) + 1], s_u))):
                    if u >= 2:
                        pe.wait_ge(s_gel if w == 0 else s_act, u - 1)
                    col = slice(256 * w + P * nib, 256 * w + P * nib + P)
                    three(out[:, :],
                          lambda c: Wh[j % RW][:, c, col], lambda c: Wl[j % RW][:, c, col],
                          lambda c: xTh[:, c, HALF * g:HALF * g + HALF],
                          lambda c: xTl[:, c, HALF * g:HALF * g + HALF], range(2)).then_inc(signal, 1)

            def down(u):
                j, nib, g = ORDER[u]
                if (j, nib) == (0, 0):
                    if g == 0:
                        pe.wait_ge(s_och, 4 * B)
                    else:
                        pe.wait_ge(s_x1, B)
                        pe.wait_ge(s_qx, 2 * B)
                        pe.wait_ge(s_ytl, B)
                if u < UNITS - 1:
                    pe.wait_ge(s_il, u + 1)
                else:
                    pe.wait_ge(s_il_last, 1)
                for tt in range(4):
                    b = 4 * g + tt
                    out = bank[4 + b // 2][:, D * (b % 2):D * (b % 2) + D]
                    t = slice(P * tt, P * tt + P)
                    for n, (a, w) in enumerate(((ih, Wh), (ih, Wl), (il, Wh))):
                        last = mmul(out, a[:, u % IR, t], w[j % RW][:, nib, 512:768],
                                    start=((j, nib) == (0, 0) and tt % 2 == 0 and n == 0),
                                    stop=((j, nib) == (STEPS - 1, 1) and n == 2),
                                    skip_group_check=True)
                    if tt == 3 or tt == 1 and u == UNITS - 1:
                        last.then_inc(s_down, 1)

            for t in range(TICKS):
                for h in conv_heads(t):
                    convolve(h, 0)
                for h in conv_heads(t):
                    convolve(h, 1)
                for b in batch(t, T_RT):
                    take(6, s_x2, b + 1)
                    pe.wait_ge(s_r, 2 * b + 2)
                    pe.wait_ge(s_x1, b + 1)
                    mmul(bank[6][:, 0:D], ident[:, :], X[:, b, :], start=True, stop=False, skip_group_check=True)
                    for c in range(2):
                        last = mmul(bank[6][:, P * c:P * c + P],
                                    R[:, b % 2, H * c:H * c + H, :].rearrange("p h i -> p (h i)"),
                                    ident[:, :], start=False, stop=(c == 1), skip_group_check=True)
                    last.then_inc(s_rt, 1)
                for b, g in group(t, T_SCORES):
                    if g == 0 and b % 4 == 0:
                        for k in range(2):
                            pe.wait_ge(s_pack[b // 4][k], 64)
                    scores(b, g)
                for b in batch(t, T_OT):
                    take(7, s_ott, b + 1)
                    pe.wait_ge(s_och, 4 * b + 4)
                    for c in range(2):
                        last = t_.transpose(bank[7][:, P * c:P * c + P], o_sb[:, b % 2, P * c:P * c + P],
                                            ident[:, :])
                    last.then_inc(s_ot, 1)
                for b, g in group(t, T_ST):
                    if g == 0:
                        pe.wait_ge(s_mt, b + 1)
                    scores_t(b, g)
                for b in batch(t, T_MPT):
                    take(7, s_mt, b + 1)
                    pe.wait_ge(s_mch, 5 * b + 5)
                    t_.transpose(bank[7][:, 0:64].bitcast(BF16)[0:112, :], mp[:, b % 2, :],
                                 identb[:, :]).then_inc(s_mpt, 1)
                for b in batch(t, T_QT):
                    take(7, s_qx, 2 * b + 2)
                    pe.wait_ge(s_xn[1], b + 1)
                    for c in range(2):
                        last = t_.transpose(bank[7][:, P * c:P * c + P], XN[:, b, P * c:P * c + P], ident[:, :])
                    last.then_inc(s_qt, 1)
                for b in batch(t, T_PROJ):
                    take(7, s_x1, b + 1)
                    pe.wait_ge(s_ott, b + 1)
                    if b == 0:
                        pe.wait_ge(s_w[3], 16)
                    for c in range(2):
                        last = mmul(bank[7][:, 0:D], oT[:, b % 2, c, :], wo[:, c, :], start=(c == 0), stop=(c == 1))
                    last.then_inc(s_proj, 1)
                for b in batch(t, T_YT):
                    take(6, s_ytl, b + 1)
                    pe.wait_ge(s_xn[2], b + 1)
                    for c in range(2):
                        last = t_.transpose(bank[6][:, P * c:P * c + P], XN[:, b, c::2], ident[:, :])
                    last.then_inc(s_yt, 1)
                for b in batch(t, T_TOK):
                    pe.wait_ge(s_pvs, b + 1)
                    for g in range(4):
                        last = t_.transpose(bank[4 + b % 2][:, P * g:P * g + P], pvs[:, b % 2, P * g:P * g + P],
                                            ident[:, :])
                    last.then_inc(s_tok, 1)
                    take(6, s_och, 4 * b + 1)
                    mmul(bank[6][:, 0:272], later[:, :], vaug[:, b, :, 0:DH + 1],
                         start=True, stop=True).then_inc(s_suf, 1)
                for u in early_units(t):
                    gate_and_up(u)
                    if u >= 2:
                        down(u - 2)
                for b, g in group(t, T_ATT):
                    attend(b, g)
            for u in range(2 * EARLY, UNITS):
                gate_and_up(u)
                down(u - 2)
            down(UNITS - 2)
            down(UNITS - 1)


def kernel(x, ctx_2048, L0_attn_Wq, L0_attn_Wk, L0_attn_Wv, L0_attn_Wo, L0_xattn_ssm_kernel, L0_xattn_D,
           L0_ffn_gate_W_packed, L0_ffn_gate_scales, L0_ffn_up_W_packed, L0_ffn_up_scales,
           L0_ffn_down_W_packed, L0_ffn_down_scales):
    import numpy as np
    import concourse.bacc as bacc
    from concourse.bass_utils import run_bass_kernel_spmd

    def arr(a):
        return np.asarray(a)

    def regroup(a, axis):
        a = arr(a)
        a = np.moveaxis(a, axis, 0)
        a = a.reshape(2, 4, 2, DH, D).transpose(0, 2, 1, 3, 4).reshape(D, D)
        return np.moveaxis(a, 0, axis)

    keys = arr(ctx_2048).transpose(2, 0, 1).reshape(2, P, B, H, HD)[:, ::-1]
    keys = np.concatenate([keys, keys[..., :4]], axis=-1)

    wqkv = np.stack([arr(L0_attn_Wq), arr(L0_attn_Wk), regroup(L0_attn_Wv, 1)])
    wo = regroup(L0_attn_Wo, 0)
    kernel_rows = np.zeros((H, 384), np.float32)
    kernel_rows[:, 128:] = arr(L0_xattn_ssm_kernel)

    def by_step(rows):
        k = rows.shape[1]
        return rows.reshape(STEPS, P, 2, k).transpose(0, 3, 2, 1).reshape(STEPS, k, 2 * P)

    down_codes = arr(L0_ffn_down_W_packed).T.reshape(STEPS, P, D)
    codes = np.concatenate([by_step(arr(L0_ffn_gate_W_packed)), by_step(arr(L0_ffn_up_W_packed)), down_codes],
                           axis=2)
    gu_scale = np.concatenate([by_step(arr(L0_ffn_gate_scales)), by_step(arr(L0_ffn_up_scales))], axis=2)
    down_scale = arr(L0_ffn_down_scales).T

    nc = bacc.Bacc("TRN2", target_bir_lowering=False, num_devices=1)
    named = [("x", arr(x)), ("ctx", keys), ("wqkv", wqkv), ("wo", wo), ("ker", kernel_rows),
             ("skip", arr(L0_xattn_D)), ("gu_scale", gu_scale), ("down_scale", down_scale), ("codes", codes)]
    arrays, args = {}, []
    for name, a in named:
        a = np.ascontiguousarray(a)
        arrays[f"in_{name}"] = a
        args.append(nc.dram_tensor(f"in_{name}", a.shape, mybir.dt.from_np(a.dtype), kind="ExternalInput").ap())
    out = nc.dram_tensor("out", (B, P, D), F32, kind="ExternalOutput").ap()
    build(nc, *args, out)
    r = run_bass_kernel_spmd(nc, [arrays], core_ids=[0])
    return r.results[0]["out"]
```
